# Optimizing a Trainium2 kernel written in Bass

```python
import numpy as np
import jax
import jax.numpy as jnp

def _softmax(x, axis=-1):
    return jax.nn.softmax(x, axis=axis)

def _gelu(x):
    return jax.nn.gelu(x, approximate=True)

def _silu(x):
    return jax.nn.silu(x)

def _sigmoid(x):
    return jax.nn.sigmoid(x)

def _layernorm(x, axis=-1, eps=1e-05):
    m = jnp.mean(x, axis=axis, keepdims=True)
    v = jnp.var(x, axis=axis, keepdims=True)
    return (x - m) / jnp.sqrt(v + eps)

def _scatter_add(tgt, idx, src, axis=0):
    return tgt.at[idx].add(src)

def _segment_sum(src, seg, n):
    return jax.ops.segment_sum(src, seg, n)
kernel_name = 'mk_gnn_preln_d4_gnn_r32_ca0c15'

def setup_inputs(seed: int=0):
    np.random.seed(seed)
    _w = jnp.asarray

    def _rec_inputs():
        import jax
        import jax.numpy as jnp
        _gk = jax.random.key(seed)
        x = -0.0002117 + 1 * jax.random.normal(jax.random.fold_in(_gk, 1), (3125, 256), jnp.float32)
        _s = jax.random.randint(jax.random.fold_in(_gk, 2), (25000,), 0, 3125, jnp.int32)
        _d = jax.random.randint(jax.random.fold_in(_gk, 3), (25000,), 0, 3125, jnp.int32)
        _loop = jnp.arange(3125, dtype=jnp.int32)
        src = jnp.concatenate([_s, _d, _loop])
        dst = jnp.concatenate([_d, _s, _loop])
        _o = jnp.argsort(dst, stable=True)
        src = src[_o]
        dst = dst[_o]
        edge_attr_64 = 0.000312547 + 1.00004 * jax.random.normal(jax.random.fold_in(_gk, 12), (53125, 64), jnp.float32)
        return (x, src, dst, edge_attr_64)
    x, src, dst, edge_attr_64 = _rec_inputs()

    def _L0_gnn_setup():
        import jax, jax.numpy as jnp
        import numpy as np
        N = 3125
        E = 25000
        EMB = 256
        HID = 256
        EPS = 1e-05

        def _pool_max(h, edge_src, edge_dst):
            pooled = jax.ops.segment_max(h[edge_src], edge_dst, num_segments=N)
            cnt = jax.ops.segment_sum(jnp.ones((edge_dst.shape[0],), h.dtype), edge_dst, num_segments=N)
            return jnp.where((cnt > 0)[:, None], pooled, jnp.zeros((), h.dtype))

        def _layernorm(x, g, b):
            mu = jnp.mean(x, axis=-1, keepdims=True)
            var = jnp.mean(jnp.square(x - mu), axis=-1, keepdims=True)
            return (x - mu) * jax.lax.rsqrt(var + EPS) * g + b
        key = jax.random.key(seed)
        ks = jax.random.split(key, 12)
        s = 0.05
        return {'embeddings': jax.random.normal(ks[0], (N, EMB), jnp.float32), 'edge_src': jax.random.randint(ks[1], (E,), 0, N, jnp.int32), 'edge_dst': jax.random.randint(ks[2], (E,), 0, N, jnp.int32), 'Wp1': jax.random.normal(ks[3], (HID, EMB), jnp.float32) * s, 'bp1': jnp.zeros((HID,), jnp.float32), 'Wm1': jax.random.normal(ks[4], (HID, EMB + HID), jnp.float32) * s, 'bm1': jnp.zeros((HID,), jnp.float32), 'Wm2': jax.random.normal(ks[5], (HID, 2 * HID), jnp.float32) * s, 'bm2': jnp.zeros((HID,), jnp.float32), 'Wm3': jax.random.normal(ks[6], (HID, 2 * HID), jnp.float32) * s, 'bm3': jnp.zeros((HID,), jnp.float32), 'ln2_g': jnp.ones((HID,), jnp.float32), 'ln2_b': jnp.zeros((HID,), jnp.float32), 'ln3_g': jnp.ones((HID,), jnp.float32), 'ln3_b': jnp.zeros((HID,), jnp.float32)}
    _L0_gnn_all = _L0_gnn_setup()
    _L0_gnn_in = {k: v for k, v in _L0_gnn_all.items() if k in ('Wp1', 'bp1', 'Wm1', 'bm1', 'Wm2', 'bm2', 'Wm3', 'bm3', 'ln2_g', 'ln2_b', 'ln3_g', 'ln3_b')}
    del _L0_gnn_all

    def _L1_gnn_setup():
        import jax, jax.numpy as jnp
        import numpy as np
        N_NODES = 3125
        N_EDGES = 10000
        D_MODEL = 256
        D_Q = D_MODEL // 16
        key = jax.random.key(seed)
        k1, k2, k3, k4 = jax.random.split(key, 4)
        Xe = jax.random.normal(k1, (N_NODES, D_MODEL), dtype=jnp.float32)
        src = jax.random.randint(k2, (N_EDGES,), 0, N_NODES, dtype=jnp.int64)
        dst = jax.random.randint(k3, (N_EDGES,), 0, N_NODES, dtype=jnp.int64)
        W_dis = jax.random.normal(k4, (D_Q, D_MODEL), dtype=jnp.float32) * (1.0 / np.sqrt(D_MODEL))
        return {'Xe': Xe, 'src': src, 'dst': dst, 'W_dis': W_dis}
    _L1_gnn_all = _L1_gnn_setup()
    _L1_gnn_in = {k: v for k, v in _L1_gnn_all.items() if k in ('W_dis',)}
    del _L1_gnn_all

    def _L2_gnn_setup():
        import jax, jax.numpy as jnp
        import numpy as np
        N, E, D_IN, D_OUT = (50000, 50000, 256, 256)
        key = jax.random.key(seed)
        k1, k2, k3, k4, k5, k6 = jax.random.split(key, 6)
        x = jax.random.normal(k1, (N, D_IN), dtype=jnp.float32)
        edge_index = jax.random.randint(k2, (2, E), 0, N, dtype=jnp.int64)
        s = 1.0 / np.sqrt(D_IN)
        W1 = jax.random.uniform(k3, (D_OUT, D_IN), minval=-s, maxval=s, dtype=jnp.float32)
        b1 = jax.random.uniform(k4, (D_OUT,), minval=-s, maxval=s, dtype=jnp.float32)
        W2 = jax.random.uniform(k5, (D_OUT, D_IN), minval=-s, maxval=s, dtype=jnp.float32)
        b2 = jax.random.uniform(k6, (D_OUT,), minval=-s, maxval=s, dtype=jnp.float32)
        return {'x': x, 'W1': W1, 'b1': b1, 'W2': W2, 'b2': b2, 'edge_index': edge_index}
    _L2_gnn_all = _L2_gnn_setup()
    _L2_gnn_in = {k: v for k, v in _L2_gnn_all.items() if k in ('W1', 'b1', 'W2', 'b2')}
    del _L2_gnn_all

    def _L3_gnn_setup():
        import jax, jax.numpy as jnp
        import numpy as np
        N, E, H, DE = (10000, 250000, 256, 64)
        EPS = 1e-05

        def _lin_init(k, fan_in, shape):
            s = 1.0 / np.sqrt(fan_in)
            return jax.random.uniform(k, shape, jnp.float32, -s, s)
        key = jax.random.key(seed)
        ks = jax.random.split(key, 12)
        x = jax.random.normal(ks[0], (N, H), jnp.float32)
        edge_index = jax.random.randint(ks[1], (2, E), 0, N)
        edge_attr = jax.random.normal(ks[2], (E, DE), jnp.float32)
        d_in = H + DE
        W1 = _lin_init(ks[3], d_in, (d_in, H))
        b1 = _lin_init(ks[4], d_in, (H,))
        W2 = _lin_init(ks[5], H, (H, H))
        b2 = _lin_init(ks[6], H, (H,))
        Wg = _lin_init(ks[7], d_in, (d_in, H))
        bg = _lin_init(ks[8], d_in, (H,))
        gamma = jnp.ones((H,), jnp.float32)
        beta = jnp.zeros((H,), jnp.float32)
        return {'x': x, 'edge_index': edge_index, 'edge_attr': edge_attr, 'W1': W1, 'b1': b1, 'W2': W2, 'b2': b2, 'Wg': Wg, 'bg': bg, 'gamma': gamma, 'beta': beta}
    _L3_gnn_all = _L3_gnn_setup()
    _L3_gnn_in = {k: v for k, v in _L3_gnn_all.items() if k in ('W1', 'b1', 'W2', 'b2', 'Wg', 'bg', 'gamma', 'beta')}
    del _L3_gnn_all
    return {'x': x, 'src': src, 'dst': dst, 'edge_attr_64': edge_attr_64, 'L0_gnn_Wp1': _L0_gnn_in['Wp1'], 'L0_gnn_bp1': _L0_gnn_in['bp1'], 'L0_gnn_Wm1': _L0_gnn_in['Wm1'], 'L0_gnn_bm1': _L0_gnn_in['bm1'], 'L0_gnn_Wm2': _L0_gnn_in['Wm2'], 'L0_gnn_bm2': _L0_gnn_in['bm2'], 'L0_gnn_Wm3': _L0_gnn_in['Wm3'], 'L0_gnn_bm3': _L0_gnn_in['bm3'], 'L0_gnn_ln2_g': _L0_gnn_in['ln2_g'], 'L0_gnn_ln2_b': _L0_gnn_in['ln2_b'], 'L0_gnn_ln3_g': _L0_gnn_in['ln3_g'], 'L0_gnn_ln3_b': _L0_gnn_in['ln3_b'], 'L1_gnn_W_dis': _L1_gnn_in['W_dis'], 'L2_gnn_W1': _L2_gnn_in['W1'], 'L2_gnn_b1': _L2_gnn_in['b1'], 'L2_gnn_W2': _L2_gnn_in['W2'], 'L2_gnn_b2': _L2_gnn_in['b2'], 'L3_gnn_W1': _L3_gnn_in['W1'], 'L3_gnn_b1': _L3_gnn_in['b1'], 'L3_gnn_W2': _L3_gnn_in['W2'], 'L3_gnn_b2': _L3_gnn_in['b2'], 'L3_gnn_Wg': _L3_gnn_in['Wg'], 'L3_gnn_bg': _L3_gnn_in['bg'], 'L3_gnn_gamma': _L3_gnn_in['gamma'], 'L3_gnn_beta': _L3_gnn_in['beta']}

def reference(x, src, dst, edge_attr_64, L0_gnn_Wp1, L0_gnn_bp1, L0_gnn_Wm1, L0_gnn_bm1, L0_gnn_Wm2, L0_gnn_bm2, L0_gnn_Wm3, L0_gnn_bm3, L0_gnn_ln2_g, L0_gnn_ln2_b, L0_gnn_ln3_g, L0_gnn_ln3_b, L1_gnn_W_dis, L2_gnn_W1, L2_gnn_b1, L2_gnn_W2, L2_gnn_b2, L3_gnn_W1, L3_gnn_b1, L3_gnn_W2, L3_gnn_b2, L3_gnn_Wg, L3_gnn_bg, L3_gnn_gamma, L3_gnn_beta):
    import jax
    import jax.numpy as jnp

    def _L0_gnn_ref(embeddings, edge_src, edge_dst, Wp1, bp1, Wm1, bm1, Wm2, bm2, Wm3, bm3, ln2_g, ln2_b, ln3_g, ln3_b):
        import jax, jax.numpy as jnp
        import numpy as np
        N = 3125
        E = 25000
        EMB = 256
        HID = 256
        EPS = 1e-05

        def _pool_max(h, edge_src, edge_dst):
            pooled = jax.ops.segment_max(h[edge_src], edge_dst, num_segments=N)
            cnt = jax.ops.segment_sum(jnp.ones((edge_dst.shape[0],), h.dtype), edge_dst, num_segments=N)
            return jnp.where((cnt > 0)[:, None], pooled, jnp.zeros((), h.dtype))

        def _layernorm(x, g, b):
            mu = jnp.mean(x, axis=-1, keepdims=True)
            var = jnp.mean(jnp.square(x - mu), axis=-1, keepdims=True)
            return (x - mu) * jax.lax.rsqrt(var + EPS) * g + b
        h1 = jax.nn.relu(embeddings @ Wp1.T + bp1)
        p1 = _pool_max(h1, edge_src, edge_dst)
        x = jax.nn.relu(jnp.concatenate([embeddings, p1], axis=1) @ Wm1.T + bm1)
        p2 = _pool_max(x, edge_src, edge_dst)
        y2 = jax.nn.relu(jnp.concatenate([x, p2], axis=1) @ Wm2.T + bm2)
        x = _layernorm(y2 + x, ln2_g, ln2_b)
        p3 = _pool_max(x, edge_src, edge_dst)
        y3 = jax.nn.relu(jnp.concatenate([x, p3], axis=1) @ Wm3.T + bm3)
        x = _layernorm(y3 + x, ln3_g, ln3_b)
        return x

    def _L1_gnn_ref(Xe, src, dst, W_dis):
        import jax, jax.numpy as jnp
        import numpy as np
        N_NODES = 3125
        N_EDGES = 10000
        D_MODEL = 256
        D_Q = D_MODEL // 16
        n_nodes = Xe.shape[0]
        q = Xe @ W_dis.T * 0.25
        E = jnp.sum(q[src] * q[dst], axis=-1)
        aij = jax.nn.relu(E)
        rij = jax.nn.relu(-E)
        A_sum = jax.ops.segment_sum(aij, dst, num_segments=n_nodes)
        R_sum = jax.ops.segment_sum(rij, dst, num_segments=n_nodes)
        XeA_sum = jax.ops.segment_sum(Xe[src] * aij[:, None], dst, num_segments=n_nodes)
        denom = A_sum + R_sum + 0.01
        Xe_trans = (XeA_sum + Xe * R_sum[:, None]) / denom[:, None]
        return Xe_trans

    def _L2_gnn_ref(x, W1, b1, W2, b2, edge_index):
        import jax, jax.numpy as jnp
        import numpy as np
        N, E, D_IN, D_OUT = (50000, 50000, 256, 256)
        dst = edge_index[0]
        nbr = edge_index[1]
        n = x.shape[0]
        agg = jax.ops.segment_sum(x[nbr], dst, num_segments=n)
        cnt = jax.ops.segment_sum(jnp.ones((nbr.shape[0],), x.dtype), dst, num_segments=n)
        mean = agg / jnp.maximum(cnt, 1.0)[:, None]
        return x @ W1.T + b1 + mean @ W2.T + b2

    def _L3_gnn_ref(x, edge_index, edge_attr, W1, b1, W2, b2, Wg, bg, gamma, beta):
        import jax, jax.numpy as jnp
        import numpy as np
        N, E, H, DE = (10000, 250000, 256, 64)
        EPS = 1e-05

        def _lin_init(k, fan_in, shape):
            s = 1.0 / np.sqrt(fan_in)
            return jax.random.uniform(k, shape, jnp.float32, -s, s)
        src, dst = (edge_index[0], edge_index[1])
        ei = jnp.concatenate([x[src], edge_attr], axis=-1)
        core = jnp.maximum(ei @ W1 + b1, 0.0) @ W2 + b2
        gate = jax.nn.sigmoid(ei @ Wg + bg)
        msg = gate * core
        agg = jax.ops.segment_sum(msg, dst, num_segments=x.shape[0])
        out = agg + x
        mu = jnp.mean(out, axis=-1, keepdims=True)
        var = jnp.var(out, axis=-1, keepdims=True)
        out = (out - mu) * jax.lax.rsqrt(var + EPS) * gamma + beta
        return out
    edge_index = jnp.stack([src, dst])
    h = jnp.maximum(_layernorm(x, axis=-1), 0.0)
    x = x + _L0_gnn_ref(h, src, dst, L0_gnn_Wp1, L0_gnn_bp1, L0_gnn_Wm1, L0_gnn_bm1, L0_gnn_Wm2, L0_gnn_bm2, L0_gnn_Wm3, L0_gnn_bm3, L0_gnn_ln2_g, L0_gnn_ln2_b, L0_gnn_ln3_g, L0_gnn_ln3_b)
    h = jnp.maximum(_layernorm(x, axis=-1), 0.0)
    x = x + _L1_gnn_ref(h, src, dst, L1_gnn_W_dis)
    h = jnp.maximum(_layernorm(x, axis=-1), 0.0)
    x = x + _L2_gnn_ref(h, L2_gnn_W1, L2_gnn_b1, L2_gnn_W2, L2_gnn_b2, edge_index)
    h = jnp.maximum(_layernorm(x, axis=-1), 0.0)
    x = x + _L3_gnn_ref(h, edge_index, edge_attr_64, L3_gnn_W1, L3_gnn_b1, L3_gnn_W2, L3_gnn_b2, L3_gnn_Wg, L3_gnn_bg, L3_gnn_gamma, L3_gnn_beta)
    return x

_drawn_inputs = setup_inputs


def setup_inputs(seed=0):
    import zlib

    import numpy as np

    out = dict(_drawn_inputs(seed))
    spreads = {'L0_gnn_bp1': (0.0, 0.1),
     'L0_gnn_bm1': (0.0, 0.1),
     'L0_gnn_bm2': (0.0, 0.1),
     'L0_gnn_bm3': (0.0, 0.1),
     'L0_gnn_ln2_g': (1.0, 0.2),
     'L0_gnn_ln2_b': (0.0, 0.1),
     'L0_gnn_ln3_g': (1.0, 0.2),
     'L0_gnn_ln3_b': (0.0, 0.1),
     'L3_gnn_gamma': (1.0, 0.2),
     'L3_gnn_beta': (0.0, 0.1)}
    factors = {'L1_gnn_W_dis': 4.104, 'L2_gnn_b1': 3.562, 'L2_gnn_b2': 3.358, 'L3_gnn_bg': 8.0}
    for name, (base, spread) in spreads.items():
        noise = np.random.default_rng([zlib.crc32(name.encode()), seed]).standard_normal(out[name].shape)
        drawn = base * np.exp(spread * noise) if base else spread * noise
        out[name] = jnp.asarray(drawn.astype(out[name].dtype))
    for name, factor in factors.items():
        out[name] = (out[name] * factor).astype(out[name].dtype)
    return out
```

```python
import concourse.bass as bass
from concourse import mybir
from contextlib import ExitStack

N_NODES, N_EDGES, D, D_EDGE, D_Q = 3125, 53125, 256, 64, 16
P = 128
TILES = (N_NODES + P - 1) // P
ROWS = TILES * P
STEPS = 416
EDGES = P * STEPS
G = 4
GROUPS = STEPS // G
OF_SLOT = [7, 6, 6, 6]
RING = 4
IDX_RING = 8
BIG = 3.0e38
EPS = 1e-5
W_TAB = [D, D, D, D + D_Q, D, 2 * D]
W_STATE = [D, D, D, D + 2, D, D]
MAX, WSUM, SUM, MLP = "max", "weighted sum", "sum", "gated mlp"
KIND = [MAX, MAX, MAX, WSUM, SUM, MLP]
STAGE_IN = [1, 2, 2, 2, 1, 2, 1]
STAGE_W = [D, D, D, D, D_Q, D, 2 * D]
M_PROJ, M_L0A, M_L0B, M_L0C, M_Q, M_SAGE, M_EDGE = range(7)
BY_DVE = (M_L0B, M_L0C, M_SAGE)
WGT_AT = [0, 2, 6, 10, 14, 18, 22]


def build(nc, dram, out):
    f32, i32, bf16 = mybir.dt.float32, mybir.dt.int32, mybir.dt.bfloat16
    ALU, ACT, AX = mybir.AluOpType, mybir.ActivationFunctionType, mybir.AxisListType
    ds = bass.ds

    ctx = ExitStack()
    with ctx:
        def sb(name, shape, dt=f32):
            return ctx.enter_context(nc.sbuf_tensor(name, shape, dt))

        def sem(name):
            return ctx.enter_context(nc.semaphore(name))

        X = sb("X", [P, TILES * D])
        H = sb("H", [P, TILES * D])
        PG_W = STEPS * D_Q
        PG = sb("PG", [P, PG_W])
        ring = sb("ring", [P, RING * G, 2 * D])
        state = sb("state", [P, RING * G, D + 2])
        work = sb("work", [P, 5120])
        wgt = sb("wgt", [P, 18, D])
        wq = sb("wq", [P, 2, D_Q])
        wedge = sb("wedge", [P, 2, 2 * D])
        wattr = sb("wattr", [D_EDGE, 2 * D])
        w2 = sb("w2", [P, 2, D])
        bias = sb("bias", [1, 9 * D])
        lnw = sb("lnw", [P, 6, D])
        ident = sb("ident", [P, P])
        ones_sq = sb("ones_sq", [P, P])
        tri = sb("tri", [P, P])
        iota_lo = sb("iota_lo", [P, P], bf16)
        iota_hi = sb("iota_hi", [P, TILES], bf16)
        hot = sb("hot", [P, G, P + 32], bf16)
        zeros = sb("zeros", [P, D + 2])
        aT = sb("aT", [P, 2, 4, P])
        idx = sb("idx", [P, IDX_RING * G], i32)
        dst_prev = sb("dst_prev", [P, STEPS + 1], i32)
        dsti = dst_prev[:, 1:]
        keep_sum = sb("keep_sum", [P, STEPS])
        keep_max = sb("keep_max", [P, STEPS])
        Q = sb("Q", [P, TILES * D_Q])
        qhead = sb("qhead", [P, D_Q])
        stat = sb("stat", [P, TILES * 6])
        mv = sb("mv", [P, 2, TILES])
        sd = sb("sd", [P, TILES])
        rstd = sb("rstd", [P, TILES])
        nmr = sb("nmr", [P, TILES])
        cnt = sb("cnt", [P, TILES])
        tmp = sb("tmp", [P, 8, 32])
        some = sb("some", [P, TILES])
        end_i = sb("end_i", [P, TILES], i32)
        start_i = sb("start_i", [P, TILES], i32)
        head_i = sb("head_i", [P, 1], i32)
        icnt = sb("icnt", [P, TILES])
        pcol = sb("pcol", [P, 4])
        eps_t = sb("eps_t", [P, 1])
        chain_sum = sb("chain_sum", [P, P])
        chain_max = sb("chain_max", [P, P])
        cont_max = sb("cont_max", [P, 1])
        cont_sum = sb("cont_sum", [P, 1])
        carryT = sb("carryT", [P, 3, P + 1])
        headrow = sb("headrow", [P, D + 2])
        mend = sb("mend", [P, D + 2])
        rn = sb("rn", [P, TILES])

        weighted = work[:, 0:RING * G * (D + 2)].rearrange("p (s w) -> p s w", w=D + 2)
        dst_lo, dst_hi = work[:, 2048:2048 + STEPS], work[:, 2560:2560 + STEPS]
        qprod = work[:, 4128:4128 + 2 * G * D_Q].rearrange("p (s w) -> p s w", w=D_Q)
        edot = work[:, 4256:4256 + 2 * G]
        zed = work[:, 0:4 * 512].rearrange("p (s w) -> p s w", w=512)
        hidT = work[:, 2048:2048 + 512].rearrange("p (s c n) -> p s c n", s=2, n=P)
        msg = work[:, 2560:2560 + 512].rearrange("p (s w) -> p s w", w=D)
        attr = work[0:D_EDGE, 3072:3072 + 4 * G * P].rearrange("p (s w) -> p s w", w=G * P)

        tp = [ctx.enter_context(nc.psum_tensor(f"tp{i}", [P, 512], f32)) for i in range(2)]
        mm = [ctx.enter_context(nc.psum_tensor(f"mm{i}", [P, 512], f32)) for i in range(2)]
        core = [ctx.enter_context(nc.psum_tensor(f"core{i}", [P, 512], f32)) for i in range(2)]
        tailT = ctx.enter_context(nc.psum_tensor("tailT", [P, 512], f32))
        tailU = ctx.enter_context(nc.psum_tensor("tailU", [P, 512], f32))

        x_in, small_in, dst_in, w_in = sem("x_in"), sem("small_in"), sem("dst_in"), sem("w_in")
        consts = sem("consts")
        zero_out = sem("zero_out")
        masks_done = sem("masks_done")
        prep_step = sem("prep_step")
        idx_in = [sem(f"idx_in{i}") for i in range(IDX_RING)]
        rows_in = [sem(f"rows_in{i}") for i in range(RING)]
        state_done = sem("state_done")
        dumped = [sem(f"dumped{i}") for i in range(RING)]
        hot_done, hot_used = sem("hot_done"), sem("hot_used")
        count_done, rank_done = sem("count_done"), sem("rank_done")
        count_here = sem("count_here")
        positions = sem("positions")
        chain_row, chain_rhs = sem("chain_row"), sem("chain_rhs")
        tail_T, tail_scan, tail_U = sem("tail_T"), sem("tail_scan"), sem("tail_U")
        head_in, head_out, mended = sem("head_in"), sem("head_out"), sem("mended")
        pooled_in = [sem(f"pooled_in{i}") for i in range(4)]
        qslot_out, qhead_in, qedge_in = sem("qslot_out"), sem("qhead_in"), sem("qedge_in")
        qhead_set, qedge_scan = sem("qhead_set"), sem("qedge_scan")
        tp_ready, at_ready, mm_ready, mm_used = (sem(n) for n in ("tp_ready", "at_ready", "mm_ready", "mm_used"))
        out_act, out_dve = sem("out_act"), sem("out_dve")
        stats_done = sem("stats_done")
        node_step = sem("node_step")
        var_ready, sd_ready, norm_ready = sem("var_ready"), sem("sd_ready"), sem("norm_ready")
        h_norm = sem("h_norm")
        tab_out = [sem(f"tab_out{i}") for i in range(5)]
        tab5_out = [sem(f"tab5_out{i}") for i in range(4)]
        mean_ready = sem("mean_ready")
        dot_step, dot_done, wrow_done = sem("dot_step"), sem("dot_done"), sem("wrow_done")
        z_ready, z_done, sig_done = sem("z_ready"), sem("z_done"), sem("sig_done")
        hT_ready, hT_done, core_ready, msg_done = (sem(n) for n in ("hT_ready", "hT_done", "core_ready", "msg_done"))
        attr_in = [sem(f"attr_in{i}") for i in range(4)]
        pace = sem("pace")
        y_out = sem("y_out")

        block = ctx.enter_context(nc.Block())

        def col(t, k, w, n=None):
            n = w if n is None else n
            return t[:, k * w:k * w + n] if isinstance(k, int) else t[:, ds(k * w, n)]

        def wait(eng, s, v):
            if isinstance(v, int):
                if v > 0:
                    eng.wait_ge(s, v)
            else:
                eng.wait_ge(s, v)
                eng.sem_inc(pace)

        def tiles(eng, body):
            for k in range(4):
                body(k, k)
            with eng.Fori(1, TILES // 4) as r:
                for i in range(4):
                    body(r * 4 + i, i)
            body(TILES - 1, 0)

        def groups(eng, body, unroll):
            for g in range(unroll):
                body(g, g)
            with eng.Fori(1, GROUPS // unroll) as r:
                for i in range(unroll):
                    body(r * unroll + i, i)

        def consumer(m):
            return (mm_used if m in BY_DVE else out_act), TILES * sum((i in BY_DVE) == (m in BY_DVE) for i in range(m))

        def used_rows(ps, g):
            return (z_done, g * G) if KIND[ps] == MLP else (state_done, ps * STEPS + g * G)

        def state_rows(ps):
            t = dram["states_wide"] if W_STATE[ps] > D else dram["states"]
            return t

        @block.sync
        def _(sp):
            sp.dma_start(X[:, :].rearrange("p (k w) -> p k w", w=D),
                         dram["x"].rearrange("(k p) w -> p k w", p=P)).then_inc(x_in, 16)
            sp.dma_start(dst_prev[:, :], dram["dst"]).then_inc(dst_in, 16)
            sp.dma_start(bias[:, :], dram["bias"]).then_inc(small_in, 16)
            sp.dma_start(wgt[:, 0:2, :], dram["w_proj"]).then_inc(small_in, 16)
            for at, name in ((2, "w_l0a"), (6, "w_l0b"), (10, "w_l0c"), (14, "w_sage")):
                sp.dma_start(wgt[:, at:at + 4, :], dram[name]).then_inc(w_in, 16)
            for t, name in ((wq[:, :, :], "w_q"), (wedge[:, :, :], "w_edge"), (wattr[:, :], "w_attr"), (w2[:, :, :], "w_2")):
                sp.dma_start(t, dram[name]).then_inc(w_in, 16)
            for i in range(6):
                sp.dma_start(lnw[:, i, :], dram["ln"][i:i + 1, :].to_broadcast([P, D])).then_inc(w_in, 16)
            wait(sp, consts, 1)
            sp.dma_start(dram["states"][EDGES:EDGES + 1, :], zeros[0:1, 0:D]).then_inc(zero_out, 16)
            sp.dma_start(dram["states_wide"][EDGES:EDGES + 1, :], zeros[0:1, :]).then_inc(zero_out, 16)
            for i in range(2 * D_Q):
                half = STEPS // 2 * D_Q // D_Q
                sp.dma_start(dram["q_edge"][0:EDGES, :].rearrange("(p t) w -> p (t w)", t=STEPS)[:, i * half:(i + 1) * half],
                             zeros[:, 0:half]).then_inc(zero_out, 16)

            def table(ps, src, width, s, first, at=0):
                def body(k, slot):
                    wait(sp, s, first + k + 1)
                    rows = dram[f"table{ps}"][k * P:(k + 1) * P, at:at + width] if isinstance(k, int) \
                        else dram[f"table{ps}"][ds(k * P, P), at:at + width]
                    sp.dma_start(rows, col(src, k, width)).then_inc(tab_out[ps], 16)
                tiles(sp, body)

            def spool(ps):
                w = W_STATE[ps]
                rows = state_rows(ps)[0:EDGES, :].rearrange("(p t) w -> p (t w)", t=STEPS)
                per = GROUPS // IDX_RING

                def dump(g, slot):
                    wait(sp, state_done, ps * STEPS + g * G + G)
                    piece = rows[:, g * G * w:(g + 1) * G * w] if isinstance(g, int) else rows[:, ds(g * (G * w), G * w)]
                    sp.dma_start(piece.rearrange("p (t w) -> p t w", w=w),
                                 state[:, slot * G:slot * G + G, 0:w]).then_inc(dumped[slot], 16)

                def load_idx(g, slot):
                    piece = dram["src"][g] if isinstance(g, int) else dram["src"][ds(g, 1)].rearrange("a p k -> (a p) k")
                    sp.dma_start(idx[:, slot * G:slot * G + G], piece).then_inc(idx_in[slot], 16)

                def load_attr(g, slot):
                    piece = dram["attr"][g] if isinstance(g, int) else dram["attr"][ds(g, 1)].rearrange("a p k -> (a p) k")
                    sp.dma_start(attr[:, slot, :], piece).then_inc(attr_in[slot], 16)

                for g in range(IDX_RING):
                    load_idx(g, g)
                if KIND[ps] == MLP:
                    for g in range(RING):
                        load_attr(g, g)
                last = GROUPS - IDX_RING

                def body(g, slot):
                    dump(g, slot % RING)
                    if KIND[ps] == MLP:
                        wait(sp, z_ready, g * G + G)
                        load_attr(g + RING, slot % RING)
                    wait(sp, *used_rows(ps, g + 1))
                    load_idx(g + IDX_RING, slot)
                for g in range(IDX_RING):
                    body(g, g)
                with sp.Fori(1, per - 1) as r:
                    for i in range(IDX_RING):
                        body(r * IDX_RING + i, i)
                for g in range(last, GROUPS):
                    dump(g, g % RING)
                    if KIND[ps] == MLP and g + RING < GROUPS:
                        wait(sp, z_ready, g * G + G)
                        load_attr(g + RING, g % RING)

            table(0, PG, D, out_act, 0)
            spool(0)
            table(1, H, D, out_act, TILES)
            spool(1)
            table(2, H, D, out_dve, 0)
            spool(2)
            table(3, H, D, h_norm, TILES)
            table(3, Q, D_Q, out_act, 2 * TILES, at=D)

            def q_table(k, slot):
                rows = dram["q_node"][k * P:(k + 1) * P, :] if isinstance(k, int) else dram["q_node"][ds(k * P, P), :]
                sp.dma_start(rows, col(Q, k, D_Q)).then_inc(tab_out[3], 16)
            tiles(sp, q_table)
            wait(sp, qslot_out, 16 * TILES)
            sp.dma_start(PG[:, :], dram["q_edge"][0:EDGES, :].rearrange("(p t) w -> p (t w)", t=STEPS)).then_inc(qedge_in, 16)
            spool(3)
            table(4, H, D, h_norm, 2 * TILES)
            spool(4)

            def edge_table(k, slot):
                wait(sp, out_act, 3 * TILES + k + 1)
                rows = dram["table5"][k * P:(k + 1) * P, :] if isinstance(k, int) else dram["table5"][ds(k * P, P), :]
                sp.dma_start(rows, ring[:, slot, :]).then_inc(tab5_out[slot], 16)
            tiles(sp, edge_table)
            spool(5)

            def result(k, slot):
                wait(sp, out_dve, TILES + k + 1)
                rows = out[k * P:(k + 1) * P, :] if isinstance(k, int) else out[ds(k * P, P), :]
                sp.dma_start(rows, col(X, k, D)).then_inc(y_out, 16)
            for k in range(4):
                result(k, k)
            with sp.Fori(1, TILES // 4) as r:
                for i in range(4):
                    result(r * 4 + i, i)
            last_rows = N_NODES - (TILES - 1) * P
            wait(sp, out_dve, 2 * TILES)
            sp.dma_start(out[(TILES - 1) * P:N_NODES, :], X[0:last_rows, (TILES - 1) * D:]).then_inc(y_out, 16)
            sp.wait_ge(y_out, 16 * TILES)

        @block.gpsimd
        def _(pool):
            pool.memset(zeros[:, :], 0.0).then_inc(consts, 1)
            pool.memset(ones_sq[:, :], 1.0).then_inc(consts, 1)
            pool.memset(ident[:, :], 0.0).then_inc(consts, 1)
            pool.memset(tri[:, :], 1.0).then_inc(consts, 1)
            pool.memset(eps_t[:, :], EPS).then_inc(consts, 1)
            pool.memset(carryT[:, :, :], 0.0).then_inc(consts, 1)
            pool.iota(iota_lo[:, :], [[1, P]], base=0, channel_multiplier=0,
                      allow_small_or_imprecise_dtypes=True).then_inc(consts, 1)
            pool.iota(iota_hi[:, :], [[1, TILES]], base=0, channel_multiplier=0,
                      allow_small_or_imprecise_dtypes=True).then_inc(consts, 1)
            pool.iota(rn[:, :], [[P, TILES]], base=0, channel_multiplier=1,
                      allow_small_or_imprecise_dtypes=True).then_inc(consts, 1)
            pool.iota(pcol[:, 0:1], [[1, 1]], base=0, channel_multiplier=STEPS,
                      allow_small_or_imprecise_dtypes=True).then_inc(consts, 1)
            pool.wait_ge(consts, 10)
            pool.affine_select(out=ident[:, :], in_=ident[:, :], compare_op=ALU.not_equal, fill=1.0,
                               base=0, pattern=[[-1, P]], channel_multiplier=1).then_inc(consts, 1)
            pool.affine_select(out=tri[:, :], in_=tri[:, :], compare_op=ALU.is_ge, fill=0.0,
                               base=0, pattern=[[1, P]], channel_multiplier=-1).then_inc(consts, 1)

            def run_pass(ps):
                w = W_TAB[ps]
                count = 75 if ps == 3 else 25
                if ps == 5:
                    for slot, s in enumerate(tab5_out):
                        pool.wait_ge(s, 16 * OF_SLOT[slot])
                else:
                    pool.wait_ge(tab_out[ps], 16 * count)
                per = GROUPS // IDX_RING

                def body(g, slot):
                    base = (ps * per + 1) * 16
                    wait(pool, idx_in[slot], base if isinstance(g, int) else (g // IDX_RING) * 16 + base)
                    if not (isinstance(g, int) and g < RING):
                        wait(pool, *used_rows(ps, g - (RING - 1)))
                    rs = slot % RING
                    for i in range(G):
                        pool.indirect_dma_start(ring[:, rs * G + i, 0:w], None, dram[f"table{ps}"],
                                                bass.IndirectOffsetOnAxis(idx[:, slot * G + i:slot * G + i + 1], 0)
                                                ).then_inc(rows_in[rs], 16)
                groups(pool, body, IDX_RING)

            def finish_pass(ps):
                w = W_STATE[ps]
                t = state_rows(ps)
                for s in dumped:
                    s_per = GROUPS // RING
                    pool.wait_ge(s, 16 * s_per * (ps + 1))
                if ps == 0:
                    pool.wait_ge(positions, 2)
                pool.indirect_dma_start(headrow[:, 0:w], None, t, bass.IndirectOffsetOnAxis(head_i[:, 0:1], 0)).then_inc(head_in, 16)
                pool.wait_ge(mended, ps + 1)
                pool.indirect_dma_start(t, bass.IndirectOffsetOnAxis(head_i[:, 0:1], 0), mend[:, 0:w], None).then_inc(head_out, 16)
                pool.wait_ge(head_out, 16 * (ps + 1))
                if ps == 0:
                    pool.wait_ge(zero_out, 16 * (2 + 2 * D_Q))
                for k in range(TILES):
                    i, r = k % 4, k // 4
                    before = 16 * (ps * OF_SLOT[i] + r)
                    if before:
                        pool.wait_ge(pooled_in[i], before)
                    pool.indirect_dma_start(PG[:, k * w:k * w + w], None, t,
                                            bass.IndirectOffsetOnAxis(end_i[:, k:k + 1], 0)).then_inc(pooled_in[i], 16)

            for ps in range(6):
                if ps == 3:
                    pool.wait_ge(out_act, 3 * TILES)
                    for k in range(TILES):
                        pool.indirect_dma_start(dram["q_edge"], bass.IndirectOffsetOnAxis(start_i[:, k:k + 1], 0),
                                                Q[:, k * D_Q:(k + 1) * D_Q], None).then_inc(qslot_out, 16)
                    pool.wait_ge(tab_out[3], 16 * 75)
                    pool.indirect_dma_start(qhead[:, :], None, dram["q_node"],
                                            bass.IndirectOffsetOnAxis(dst_prev[:, 1:2], 0)).then_inc(qhead_in, 16)
                run_pass(ps)
                finish_pass(ps)

        @block.tensor
        def _(pe):
            def stage(m, ready):
                n_in, w, base = STAGE_IN[m], STAGE_W[m], m * TILES
                used, used_base = consumer(m)

                def transposes(k, slot):
                    ready(k, slot)
                    wait(pe, at_ready, base + max(k - 1, 0))
                    for s in range(n_in):
                        src = (H, PG)[s]
                        for c in range(2):
                            last = nc.tensor.transpose(tp[slot % 2][:, (2 * s + c) * P:(2 * s + c + 1) * P],
                                                       src[:, k * D + c * P:k * D + c * P + P], ident[:, :])
                    last.then_inc(tp_ready, 1)

                def multiply(k, slot):
                    wait(pe, at_ready, base + k + 1)
                    if k == 0 and m > 0:
                        before, before_base = consumer(m - 1)
                        wait(pe, before, before_base + TILES)
                    wait(pe, used, used_base + max(k - 1, 0))
                    o = mm[slot % 2][:, 0:w]
                    for c in range(2 * n_in):
                        rhs = wq[:, c, :] if m == M_Q else wedge[:, c, :] if m == M_EDGE else wgt[:, WGT_AT[m] + c if m < M_Q else 14 + c, :]
                        last = nc.tensor.matmul(o, aT[:, slot % 2, c, :], rhs, start=(c == 0),
                                                stop=(m == M_Q and c == 1))
                    rows = {M_PROJ: [0], M_L0A: [1], M_L0B: [2], M_L0C: [3], M_Q: [], M_SAGE: [4, 5], M_EDGE: [6]}[m]
                    for n, b in enumerate(rows):
                        last = nc.tensor.matmul(o, ones_sq[0:1, :], bias[0:1, b * D:b * D + w], start=False,
                                                stop=(n == len(rows) - 1))
                    last.then_inc(mm_ready, 1)

                for k in range(TILES):
                    transposes(k, k % 4)
                    if k:
                        multiply(k - 1, (k - 1) % 4)
                multiply(TILES - 1, 0)

            def pooled(ps):
                def ready(k, slot):
                    n = OF_SLOT[slot]
                    wait(pe, pooled_in[slot], (k // 4) * 16 + 16 * (ps * n + 1))
                return ready

            def counts():
                o = tailU[:, 0:TILES]
                nc.tensor.matmul(o, ones_sq[:, :], zeros[:, 0:TILES], start=True, stop=False)

                def body(g, slot):
                    wait(pe, hot_done, g * G + G)
                    for i in range(G):
                        last = nc.tensor.matmul(o, hot[:, i, 0:P], hot[:, i, P:P + TILES], start=False, stop=False)
                    last.then_inc(hot_used, 1)
                groups(pe, body, RING)
                nc.tensor.matmul(o, ones_sq[:, :], zeros[:, 0:TILES], start=False, stop=True).then_inc(count_done, 1)
                pe.wait_ge(count_here, 1)
                nc.tensor.matmul(tailU[:, 64:64 + TILES], tri[:, :], cnt[:, :], start=True, stop=True)
                nc.tensor.matmul(tailU[:, 128:128 + TILES], ones_sq[:, :], cnt[:, :], start=True, stop=True).then_inc(rank_done, 1)
                pe.wait_ge(chain_rhs, 1)
                pe.wait_ge(positions, 1)
                nc.tensor.matmul(tailU[:, 256:384], ones_sq[:, :], chain_sum[:, :], start=True, stop=True).then_inc(chain_row, 1)

            def tail(ps):
                w = W_STATE[ps]
                pe.wait_ge(state_done, STEPS * (ps + 1))
                if ps == 0:
                    pe.wait_ge(positions, 2)
                blocks = [(0, P), (P, P)] + ([(2 * P, 2)] if w > D else [])
                for b, (at, n) in enumerate(blocks):
                    last = nc.tensor.transpose(tailT[0:n, b * P:(b + 1) * P], state[:, RING * G - 1, at:at + n], ident[:, :])
                last.then_inc(tail_T, 1)
                pe.wait_ge(tail_scan, 3 * ps + 3)
                for b, (at, n) in enumerate(blocks):
                    last = nc.tensor.transpose(tailU[:, at:at + n], carryT[0:n, b, 0:P], ident[0:n, 0:n])
                last.then_inc(tail_U, 1)

            def edge_mlp():
                pe.wait_ge(out_act, 4 * TILES)

                def attr_part(t, g, slot, i):
                    if i == 0:
                        wait(pe, attr_in[slot], g // RING * 16 + 16)
                    wait(pe, z_done, t - 1)
                    nc.tensor.matmul(mm[i % 2][:, :], attr[:, slot, i * P:(i + 1) * P], wattr[:, :],
                                     start=True, stop=True).then_inc(z_ready, 1)

                def hidden_T(t, s):
                    wait(pe, z_done, t + 1)
                    wait(pe, hT_done, t - 1)
                    for c in range(2):
                        last = nc.tensor.transpose(tp[s % 2][:, c * P:(c + 1) * P], zed[:, s % 4, c * P:(c + 1) * P], ident[:, :])
                    last.then_inc(hT_ready, 1)

                def core_part(t, s):
                    wait(pe, hT_done, t + 1)
                    wait(pe, msg_done, t - 1)
                    for c in range(2):
                        nc.tensor.matmul(core[s % 2][:, 0:D], hidT[:, s % 2, c, :], w2[:, c, :], start=(c == 0), stop=False)
                    nc.tensor.matmul(core[s % 2][:, 0:D], ones_sq[0:1, :], bias[0:1, 8 * D:9 * D], start=False,
                                     stop=True).then_inc(core_ready, 1)

                def body(g, slot):
                    for i in range(G):
                        t, s = g * G + i, slot * G + i
                        attr_part(t, g, slot, i)
                        if not isinstance(t, int) or t >= 1:
                            hidden_T(t - 1, (s - 1) % 16)
                        if not isinstance(t, int) or t >= 2:
                            core_part(t - 2, (s - 2) % 16)
                groups(pe, body, RING)
                hidden_T(STEPS - 1, 15)
                core_part(STEPS - 2, 14)
                core_part(STEPS - 1, 15)

            pe.wait_ge(consts, 12)
            pe.wait_ge(small_in, 32)
            stage(M_PROJ, lambda k, slot: wait(pe, h_norm, k + 1))
            counts()
            tail(0)
            pe.wait_ge(w_in, 16 * 14)
            stage(M_L0A, pooled(0))
            tail(1)
            pe.wait_ge(out_act, 2 * TILES)
            stage(M_L0B, pooled(1))
            tail(2)
            pe.wait_ge(out_dve, TILES)
            stage(M_L0C, pooled(2))
            stage(M_Q, lambda k, slot: wait(pe, h_norm, TILES + k + 1))
            tail(3)
            pe.wait_ge(h_norm, 3 * TILES)
            tail(4)
            stage(M_SAGE, lambda k, slot: wait(pe, mean_ready, k + 1))
            stage(M_EDGE, lambda k, slot: wait(pe, h_norm, 3 * TILES + k + 1))
            edge_mlp()
            tail(5)

        @block.scalar
        def _(act):
            def stage(m, output):
                n_in, base = STAGE_IN[m], m * TILES

                def copy_T(k, slot):
                    wait(act, tp_ready, base + k + 1)
                    if isinstance(k, int):
                        wait(act, mm_ready, base + max(k - 1, 0))
                    else:
                        wait(act, mm_ready, base + k - 1)
                    nc.scalar.activation(aT[:, slot % 2, 0:2 * n_in, :],
                                         tp[slot % 2][:, 0:2 * n_in * P].rearrange("p (c n) -> p c n", n=P),
                                         ACT.Copy).then_inc(at_ready, 1)

                def body(k, slot):
                    copy_T(k, slot)
                    if output and not (isinstance(k, int) and k == 0):
                        wait(act, mm_ready, base + k)
                        output(k - 1, (slot - 1) % 4)
                tiles(act, body)
                if output:
                    wait(act, mm_ready, base + TILES)
                    output(TILES - 1, 0)

            def root(n):
                act.wait_ge(var_ready, n)
                nc.scalar.activation(sd[:, :], mv[:, 1, :], ACT.Sqrt, bias=eps_t[:, 0:1]).then_inc(sd_ready, 1)

            def normalise(n, func, src, dst):
                act.wait_ge(norm_ready, n)

                def body(k, slot):
                    rs = rstd[:, k:k + 1] if isinstance(k, int) else rstd[:, ds(k, 1)]
                    nm = nmr[:, k:k + 1] if isinstance(k, int) else nmr[:, ds(k, 1)]
                    nc.scalar.activation(col(dst, k, D), col(src, k, D), func, bias=nm, scale=rs).then_inc(h_norm, 1)
                tiles(act, body)

            def relu_to(dst):
                def output(k, slot):
                    o = nc.scalar.activation(col(dst, k, D), mm[slot % 2][:, 0:D], ACT.Relu)
                    o.then_inc(out_act, 1)
                return output

            def weigh_rows():
                def body(g, slot):
                    wait(act, dot_done, g + 1)
                    wait(act, state_done, 3 * STEPS + (g - (RING - 1)) * G if not isinstance(g, int) else (3 * STEPS + (g - (RING - 1)) * G if g >= RING else 0))
                    for i in range(G):
                        s = slot * G + i
                        last = nc.scalar.activation(weighted[:, s, 0:D], ring[:, s, 0:D], ACT.Copy,
                                                    scale=weighted[:, s, D:D + 1])
                        last.then_inc(wrow_done, 1)
                groups(act, body, RING)

            def edge_gates():
                def gate(t, s):
                    wait(act, z_done, t + 1)
                    nc.scalar.activation(zed[:, s % 4, D:2 * D], zed[:, s % 4, D:2 * D], ACT.Sigmoid).then_inc(sig_done, 1)

                def hidden(t, s):
                    wait(act, hT_ready, t + 1)
                    wait(act, core_ready, t - 1)
                    nc.scalar.activation(hidT[:, s % 2, :, :], tp[s % 2][:, 0:2 * P].rearrange("p (c n) -> p c n", n=P),
                                         ACT.Relu).then_inc(hT_done, 1)

                def body(g, slot):
                    for i in range(G):
                        t, s = g * G + i, slot * G + i
                        gate(t, s)
                        if not isinstance(t, int) or t >= 1:
                            hidden(t - 1, (s - 1) % 16)
                groups(act, body, RING)
                hidden(STEPS - 1, 15)

            act.wait_ge(consts, 12)
            root(1)
            normalise(1, ACT.Relu, X, H)
            stage(M_PROJ, relu_to(PG))
            stage(M_L0A, relu_to(H))
            stage(M_L0B, None)
            root(2)
            stage(M_L0C, None)
            root(3)
            root(4)
            normalise(4, ACT.Relu, X, H)

            def scaled_q(k, slot):
                nc.scalar.activation(col(Q, k, D_Q), mm[slot % 2][:, 0:D_Q], ACT.Copy, scale=0.25).then_inc(out_act, 1)
            stage(M_Q, scaled_q)
            weigh_rows()
            root(5)
            normalise(5, ACT.Relu, X, H)
            stage(M_SAGE, None)
            root(6)
            normalise(6, ACT.Relu, X, H)

            def staged(k, slot):
                if not (isinstance(k, int) and k < 4):
                    wait(act, tab5_out[slot], (k // 4) * 16)
                nc.scalar.activation(ring[:, slot, :], mm[slot % 2][:, :], ACT.Copy).then_inc(out_act, 1)
            stage(M_EDGE, staged)
            edge_gates()
            root(7)

        @block.vector
        def _(dve):
            v = nc.vector
            steps = [0]

            def prep(ins):
                steps[0] += 1
                ins.then_inc(prep_step, 1)
                dve.wait_ge(prep_step, steps[0])

            at = {"base": 0, "n": 0}

            def chained(ins):
                at["n"] += 1
                ins.then_inc(node_step, 1)
                wait(dve, node_step, at["base"] + at["n"])

            def chained_tiles(per, body):
                base = at["base"]

                def one(k, slot):
                    at["base"], at["n"] = base + k * per, 0
                    body(k, slot)
                    assert at["n"] == per
                tiles(dve, one)
                at["base"], at["n"] = base + TILES * per, 0

            def chained_once(ins):
                chained(ins)
                at["base"], at["n"] = at["base"] + 1, 0

            def moments(src, w, k):
                v.bn_stats(col(stat, k, 6), col(src, k, w, D)).then_inc(stats_done, 1)

            norms = [0]

            def invert():
                norms[0] += 1
                dve.wait_ge(stats_done, TILES * norms[0])
                s3 = stat[:, :].rearrange("p (k c) -> p k c", c=6)
                mean_e, dev_e, mean_o, dev_o = (s3[:, :, c] for c in (1, 2, 4, 5))
                v.tensor_tensor(mv[:, 0, :], mean_e, mean_o, ALU.add).then_inc(node_step, 1)
                v.tensor_tensor(mv[:, 1, :], dev_e, dev_o, ALU.add).then_inc(node_step, 1)
                at["base"] += 2
                chained_once(v.tensor_tensor(sd[:, :], mean_e, mean_o, ALU.subtract))
                chained_once(v.tensor_tensor(sd[:, :], sd[:, :], sd[:, :], ALU.mult))
                chained_once(v.tensor_scalar(sd[:, :], sd[:, :], 0.25, None, ALU.mult))
                chained_once(v.scalar_tensor_tensor(out=mv[:, 1, :], in0=mv[:, 1, :], scalar=1.0 / D, in1=sd[:, :],
                                                    op0=ALU.mult, op1=ALU.add))
                v.engine_nop().then_inc(var_ready, 1)
                dve.wait_ge(sd_ready, norms[0])
                chained_once(v.reciprocal(rstd[:, :], sd[:, :]))
                v.scalar_tensor_tensor(out=nmr[:, :], in0=mv[:, 0, :], scalar=-0.5, in1=rstd[:, :],
                                       op0=ALU.mult, op1=ALU.mult).then_inc(norm_ready, 1)
                dve.wait_ge(norm_ready, norms[0])

            def per_tile(t, k):
                return t[:, k:k + 1] if isinstance(k, int) else t[:, ds(k, 1)]

            dve.wait_ge(dst_in, 16)
            dve.wait_ge(consts, 12)
            prep(v.memset(keep_sum[:, 0:1], 0.0))
            prep(v.tensor_tensor(keep_sum[:, 1:], dsti[:, 1:], dsti[:, 0:STEPS - 1], ALU.is_equal))
            v.tensor_scalar(keep_max[:, :], keep_sum[:, :], -1.0, BIG, ALU.add, ALU.mult).then_inc(masks_done, 1)
            dve.wait_ge(masks_done, 1)

            dve.wait_ge(x_in, 16)
            chained_tiles(0, lambda k, slot: moments(X, D, k))
            invert()

            lo_i = work[:, 0:STEPS].bitcast(i32)
            hi_i = work[:, 512:512 + STEPS].bitcast(i32)
            eq = work[:, 1024:1024 + STEPS]
            prep(v.tensor_scalar(lo_i, dsti, P - 1, None, ALU.bitwise_and))
            prep(v.tensor_scalar(hi_i, dsti, 7, None, ALU.logical_shift_right))
            prep(v.tensor_copy(dst_lo, lo_i))
            prep(v.tensor_copy(dst_hi, hi_i))
            prep(v.tensor_copy(pcol[:, 1:2], dsti[:, 0:1]))
            prep(v.tensor_tensor(cont_sum[:, :], dsti[:, 0:1], dst_prev[:, 0:1], ALU.is_equal))
            prep(v.tensor_scalar(cont_max[:, :], cont_sum[:, :], -1.0, BIG, ALU.add, ALU.mult))
            prep(v.tensor_copy(eq, dsti))
            prep(v.tensor_scalar(eq, eq, pcol[:, 1:2], None, ALU.is_equal))
            prep(v.tensor_reduce(pcol[:, 3:4], eq, AX.X, ALU.add))
            prep(v.scalar_tensor_tensor(out=tmp[:, 0, 0:1], in0=pcol[:, 3:4], scalar=-1.0, in1=pcol[:, 0:1],
                                        op0=ALU.add, op1=ALU.add))
            prep(v.tensor_copy(head_i[:, :], tmp[:, 0, 0:1]))
            prep(v.scalar_tensor_tensor(out=tmp[:, 1, 0:1], in0=pcol[:, 3:4], scalar=float(STEPS), in1=cont_sum[:, :],
                                        op0=ALU.is_equal, op1=ALU.mult))
            v.tensor_scalar(chain_sum[:, :], ident[:, :], tmp[:, 1, 0:1], None, ALU.mult).then_inc(chain_rhs, 1)

            def scan_step(ps, t, slot, t_mask, src):
                w = W_STATE[ps]
                if isinstance(t, int) and t == 0:
                    v.tensor_copy(state[:, slot, 0:w], src).then_inc(state_done, 1)
                    return
                wait(dve, state_done, ps * STEPS + t)
                mask, op0, op1 = (keep_max, ALU.add, ALU.max) if KIND[ps] == MAX else (keep_sum, ALU.mult, ALU.add)
                v.scalar_tensor_tensor(out=state[:, slot, 0:w], in0=state[:, (slot - 1) % (RING * G), 0:w],
                                       scalar=per_tile(mask, t_mask), in1=src, op0=op0, op1=op1).then_inc(state_done, 1)

            def slot_free(ps, g, slot):
                wait(dve, dumped[slot], (ps * (GROUPS // RING) + g // RING) * 16)

            def rows_there(ps, g, slot):
                wait(dve, rows_in[slot], (ps * (GROUPS // RING) + g // RING + 1) * (16 * G))

            def scan_pass(ps):
                w = W_STATE[ps]

                def body(g, slot):
                    if ps == 0:
                        wait(dve, hot_used, g)
                        for i in range(G):
                            v.tensor_scalar(hot[:, i, 0:P], iota_lo[:, :], per_tile(dst_lo, g * G + i), None, ALU.is_equal)
                            v.tensor_scalar(hot[:, i, P:P + TILES], iota_hi[:, :], per_tile(dst_hi, g * G + i), None,
                                            ALU.is_equal).then_inc(hot_done, 1)
                    rows_there(ps, g, slot)
                    slot_free(ps, g, slot)
                    for i in range(G):
                        scan_step(ps, g * G + i, slot * G + i, g * G + i, ring[:, slot * G + i, 0:w])
                groups(dve, body, RING)

            def weighted_pass():
                ps = 3

                def dots(g, slot):
                    rows_there(ps, g, slot)
                    if not (isinstance(g, int) and g < RING):
                        wait(dve, state_done, ps * STEPS + (g - RING + 1) * G)
                    n = g * 3
                    rs = slice(slot * G, slot * G + G)
                    qd = PG[:, g * G * D_Q:(g + 1) * G * D_Q] if isinstance(g, int) else PG[:, ds(g * (G * D_Q), G * D_Q)]
                    v.tensor_tensor(qprod[:, 0:G, :], ring[:, rs, D:D + D_Q], qd.rearrange("p (t w) -> p t w", w=D_Q),
                                    ALU.mult).then_inc(dot_step, 1)
                    wait(dve, dot_step, n + 1)
                    v.tensor_reduce(edot[:, 0:G], qprod[:, 0:G, :], AX.X, ALU.add).then_inc(dot_step, 1)
                    wait(dve, dot_step, n + 2)
                    v.tensor_scalar(weighted[:, rs, D + 1], edot[:, 0:G], -1.0, 0.0, ALU.mult, ALU.max).then_inc(dot_step, 1)
                    wait(dve, dot_step, n + 3)
                    v.tensor_scalar(weighted[:, rs, D], edot[:, 0:G], 0.0, None, ALU.max).then_inc(dot_done, 1)

                def scans(g, slot):
                    slot_free(ps, g, slot)
                    for i in range(G):
                        wait(dve, wrow_done, g * G + i + 1)
                        scan_step(ps, g * G + i, slot * G + i, g * G + i, weighted[:, slot * G + i, :])

                def body(g, slot):
                    dots(g, slot)
                    if not (isinstance(g, int) and g == 0):
                        scans(g - 1, (slot - 1) % RING)
                groups(dve, body, RING)
                scans(GROUPS - 1, RING - 1)

            def mlp_pass():
                ps = 5

                def add(t, g, slot, i):
                    if i == 0:
                        rows_there(ps, g, slot)
                    s = slot * G + i
                    wait(dve, z_ready, t + 1)
                    wait(dve, msg_done, t - 3)
                    z = v.tensor_tensor(zed[:, s % 4, :], mm[s % 2][:, :], ring[:, s, :], ALU.add)
                    z.then_inc(z_done, 1)

                def message(t, g, s):
                    wait(dve, core_ready, t + 1)
                    wait(dve, sig_done, t + 1)
                    v.tensor_tensor(msg[:, s % 2, :], core[s % 2][:, 0:D], zed[:, s % 4, D:2 * D], ALU.mult).then_inc(msg_done, 1)
                    if s % G == 0:
                        slot_free(ps, g, s // G)
                    wait(dve, msg_done, t + 1)
                    scan_step(ps, t, s, t, msg[:, s % 2, :])

                def body(g, slot):
                    for i in range(G):
                        t, s = g * G + i, slot * G + i
                        add(t, g, slot, i)
                        if not isinstance(t, int) or t >= 3:
                            message(t - 3, g if i >= 3 else g - 1, (s - 3) % 16)
                groups(dve, body, RING)
                for s in (13, 14, 15):
                    message(STEPS - 16 + s, GROUPS - 1, s)

            def tail(ps):
                w = W_STATE[ps]
                wide = w > D
                row = chain_max if KIND[ps] == MAX else chain_sum
                op0, op1 = (ALU.add, ALU.max) if KIND[ps] == MAX else (ALU.mult, ALU.add)
                dve.wait_ge(tail_T, ps + 1)
                for b in range(3):
                    n = P if b < 2 else 2
                    if b == 2 and not wide:
                        v.engine_nop().then_inc(tail_scan, 1)
                        continue
                    v.tensor_tensor_scan(carryT[0:n, b, 1:P + 1], row[0:n, :], tailT[0:n, b * P:(b + 1) * P], 0.0,
                                         op0, op1).then_inc(tail_scan, 1)
                dve.wait_ge(tail_U, ps + 1)
                dve.wait_ge(head_in, 16 * (ps + 1))
                if ps:
                    dve.wait_ge(head_out, 16 * ps)
                cont = cont_max if KIND[ps] == MAX else cont_sum
                v.scalar_tensor_tensor(out=mend[:, 0:w], in0=tailU[:, 0:w], scalar=cont[:, 0:1], in1=headrow[:, 0:w],
                                       op0=op0, op1=op1).then_inc(mended, 1)

            def pooled(ps, k, slot):
                n = OF_SLOT[slot]
                wait(dve, pooled_in[slot], (k // 4) * 16 + 16 * (ps * n + 1))

            def product(m, k):
                wait(dve, mm_ready, m * TILES + k + 1)

            dve.wait_ge(prep_step, steps[0])
            scan_pass(0)
            dve.wait_ge(count_done, 1)
            v.tensor_copy(cnt[:, :], tailU[:, 0:TILES]).then_inc(count_here, 1)
            dve.wait_ge(rank_done, 1)
            total, within = tmp[:, 2, 0:TILES], tmp[:, 3, 0:TILES]
            prep(v.tensor_copy(total, tailU[:, 128:128 + TILES]))
            prep(v.tensor_copy(within, tailU[:, 64:64 + TILES]))
            prep(v.tensor_tensor_scan(tmp[:, 4, 0:TILES], ones_sq[:, 0:TILES], total, 0.0, ALU.mult, ALU.add))
            prep(v.tensor_tensor(tmp[:, 4, 0:TILES], tmp[:, 4, 0:TILES], total, ALU.subtract))
            prep(v.tensor_tensor(within, within, tmp[:, 4, 0:TILES], ALU.add))
            prep(v.tensor_scalar(some[:, :], cnt[:, :], 1.0, None, ALU.min))
            prep(v.tensor_scalar(tmp[:, 5, 0:TILES], within, float(-1 - EDGES), None, ALU.add))
            prep(v.tensor_tensor(tmp[:, 5, 0:TILES], tmp[:, 5, 0:TILES], some[:, :], ALU.mult))
            prep(v.tensor_scalar(tmp[:, 5, 0:TILES], tmp[:, 5, 0:TILES], float(EDGES), None, ALU.add))
            prep(v.tensor_copy(end_i[:, :], tmp[:, 5, 0:TILES]))
            prep(v.tensor_tensor(within, within, cnt[:, :], ALU.subtract))
            prep(v.tensor_scalar(rn[:, :], rn[:, :], float(EDGES), None, ALU.add))
            prep(v.tensor_tensor(within, within, rn[:, :], ALU.subtract))
            prep(v.tensor_tensor(within, within, some[:, :], ALU.mult))
            prep(v.tensor_tensor(within, within, rn[:, :], ALU.add))
            prep(v.tensor_copy(start_i[:, :], within))
            prep(v.tensor_scalar(icnt[:, :], cnt[:, :], 1.0, None, ALU.max))
            prep(v.reciprocal(icnt[:, :], icnt[:, :]))
            v.engine_nop().then_inc(positions, 1)
            dve.wait_ge(chain_row, 1)
            prep(v.tensor_copy(chain_sum[:, :], tailU[:, 256:384]))
            prep(v.tensor_scalar(chain_max[:, :], chain_sum[:, :], -1.0, BIG, ALU.add, ALU.mult))
            v.engine_nop().then_inc(positions, 1)
            tail(0)

            scan_pass(1)
            tail(1)

            def add_relu(m):
                def body(k, slot):
                    product(m, k)
                    v.scalar_tensor_tensor(out=col(H, k, D), in0=mm[slot % 2][:, 0:D], scalar=0.0, in1=col(H, k, D),
                                           op0=ALU.max, op1=ALU.add).then_inc(mm_used, 1)
                    wait(dve, mm_used, consumer(m)[1] + k + 1)
                    moments(H, D, k)
                chained_tiles(0, body)

            def affine(src, w, wrow, brow):
                def run(k):
                    x = col(src, k, D)
                    chained(v.tensor_scalar(x, x, per_tile(rstd, k), per_tile(nmr, k), ALU.mult, ALU.add))
                    chained(v.tensor_tensor(x, x, lnw[:, wrow, :], ALU.mult))
                return run

            dve.wait_ge(w_in, 16 * 14)
            add_relu(M_L0B)
            invert()

            def second(k, slot):
                affine(H, D, 0, 1)(k)
                v.tensor_tensor(col(H, k, D), col(H, k, D), lnw[:, 1, :], ALU.add).then_inc(out_dve, 1)
            chained_tiles(2, second)
            dve.wait_ge(out_dve, TILES)

            scan_pass(2)
            tail(2)

            add_relu(M_L0C)
            invert()

            def third(k, slot):
                affine(H, D, 2, 3)(k)
                chained(v.tensor_tensor(col(H, k, D), col(H, k, D), lnw[:, 3, :], ALU.add))
                chained(v.tensor_tensor(col(X, k, D), col(X, k, D), col(H, k, D), ALU.add))
                moments(X, D, k)
            chained_tiles(4, third)
            invert()

            qe = PG[:, :].rearrange("p (t w) -> p t w", w=D_Q)
            dve.wait_ge(qedge_in, 16)
            dve.wait_ge(qhead_in, 16)
            prep(v.tensor_copy(qe[:, 0, :], qhead[:, :]))
            for c in range(D_Q):
                prep(v.tensor_tensor_scan(qe[:, :, c], keep_sum[:, :], qe[:, :, c], 0.0, ALU.mult, ALU.add))
            weighted_pass()
            tail(3)

            w = W_STATE[3]
            for i in range(4):
                n = OF_SLOT[i]
                dve.wait_ge(pooled_in[i], 16 * 4 * n)
            pg3 = PG[:, 0:TILES * w].rearrange("p (k w) -> p k w", w=w)
            inv, rr = tmp[:, 5, 0:TILES], tmp[:, 6, 0:TILES]
            chained_once(v.scalar_tensor_tensor(out=inv, in0=pg3[:, :, D], scalar=0.01, in1=pg3[:, :, D + 1],
                                                op0=ALU.add, op1=ALU.add))
            chained_once(v.reciprocal(inv, inv))
            chained_once(v.tensor_tensor(rr, pg3[:, :, D + 1], inv, ALU.mult))

            def mix(k, slot):
                x = col(X, k, D)
                chained(v.scalar_tensor_tensor(out=x, in0=col(PG, k, w, D), scalar=per_tile(inv, k), in1=x,
                                               op0=ALU.mult, op1=ALU.add))
                chained(v.scalar_tensor_tensor(out=x, in0=col(H, k, D), scalar=per_tile(rr, k), in1=x,
                                               op0=ALU.mult, op1=ALU.add))
                moments(X, D, k)
            chained_tiles(2, mix)
            invert()

            scan_pass(4)
            tail(4)

            def mean(k, slot):
                pooled(4, k, slot)
                v.tensor_scalar(col(PG, k, D), col(PG, k, D), per_tile(icnt, k), None, ALU.mult).then_inc(mean_ready, 1)
            tiles(dve, mean)

            def sage(k, slot):
                product(M_SAGE, k)
                v.tensor_tensor(col(X, k, D), mm[slot % 2][:, 0:D], col(X, k, D), ALU.add).then_inc(mm_used, 1)
                wait(dve, mm_used, consumer(M_SAGE)[1] + k + 1)
                moments(X, D, k)
            chained_tiles(0, sage)
            invert()

            mlp_pass()
            tail(5)

            def last_sum(k, slot):
                pooled(5, k, slot)
                chained(v.tensor_tensor(col(H, k, D), col(PG, k, D), col(H, k, D), ALU.add))
                moments(H, D, k)
            chained_tiles(1, last_sum)
            invert()

            def final(k, slot):
                affine(H, D, 4, 5)(k)
                chained(v.tensor_tensor(col(H, k, D), col(H, k, D), lnw[:, 5, :], ALU.add))
                v.tensor_tensor(col(X, k, D), col(X, k, D), col(H, k, D), ALU.add).then_inc(out_dve, 1)
            chained_tiles(3, final)


def kernel(x, src, dst, edge_attr_64, **w):
    import numpy as np
    import concourse.bacc as bacc
    from concourse.bass_utils import run_bass_kernel_spmd

    def pad(a, n, value=0):
        a = np.asarray(a)
        return np.concatenate([a, np.full((n - a.shape[0],) + a.shape[1:], value, a.dtype)])

    def weights(*parts):
        a = np.concatenate([np.asarray(p) for p in parts], 0)
        return a.reshape(-1, P, a.shape[1]).transpose(1, 0, 2)

    w = {k: np.asarray(v) for k, v in w.items()}
    zero_row = np.zeros(D, np.float32)
    arrays = {
        "x": pad(x, ROWS),
        "src": pad(src, EDGES).reshape(P, GROUPS, G).transpose(1, 0, 2),
        "dst": np.lib.stride_tricks.sliding_window_view(
            pad(np.concatenate([np.full(1, -1, np.int32), np.asarray(dst)]), EDGES + 1, ROWS), STEPS + 1)[::STEPS],
        "attr": pad(edge_attr_64, EDGES).reshape(P, GROUPS, G, D_EDGE).transpose(1, 3, 2, 0).reshape(GROUPS, D_EDGE, G * P),
        "w_proj": weights(w["L0_gnn_Wp1"].T), "w_l0a": weights(w["L0_gnn_Wm1"].T),
        "w_l0b": weights(w["L0_gnn_Wm2"].T), "w_l0c": weights(w["L0_gnn_Wm3"].T),
        "w_sage": weights(w["L2_gnn_W1"].T, w["L2_gnn_W2"].T), "w_q": weights(w["L1_gnn_W_dis"].T),
        "w_edge": weights(np.concatenate([w["L3_gnn_W1"][:D], w["L3_gnn_Wg"][:D]], 1)),
        "w_attr": np.concatenate([w["L3_gnn_W1"][D:], w["L3_gnn_Wg"][D:]], 1),
        "w_2": weights(w["L3_gnn_W2"]),
        "bias": np.concatenate([w[n] for n in ("L0_gnn_bp1", "L0_gnn_bm1", "L0_gnn_bm2", "L0_gnn_bm3", "L2_gnn_b1",
                                               "L2_gnn_b2", "L3_gnn_b1", "L3_gnn_bg", "L3_gnn_b2")])[None],
        "ln": np.stack([w[n] for n in ("L0_gnn_ln2_g", "L0_gnn_ln2_b", "L0_gnn_ln3_g", "L0_gnn_ln3_b",
                                       "L3_gnn_gamma", "L3_gnn_beta")]),
    }
    arrays = {n: np.ascontiguousarray(a) for n, a in arrays.items()}
    nc = bacc.Bacc("TRN2", target_bir_lowering=False, num_devices=1)
    dram = {n: nc.dram_tensor(f"in_{n}", a.shape, mybir.dt.from_np(a.dtype), kind="ExternalInput").ap()
            for n, a in arrays.items()}
    scratch = {"states": (EDGES + 1, D), "states_wide": (EDGES + 1, D + 2), "q_edge": (EDGES + ROWS, D_Q),
               "q_node": (ROWS, D_Q)}
    scratch.update({f"table{i}": (ROWS, W_TAB[i]) for i in range(6)})
    for n, shape in scratch.items():
        dram[n] = nc.dram_tensor(n, shape, mybir.dt.float32, kind="Internal").ap()
    out = nc.dram_tensor("out", (N_NODES, D), mybir.dt.float32, kind="ExternalOutput").ap()
    build(nc, dram, out)
    r = run_bass_kernel_spmd(nc, [{f"in_{n}": a for n, a in arrays.items()}], core_ids=[0])
    return r.results[0]["out"]
```

```python
import concourse.bass as bass
from concourse import mybir
from contextlib import ExitStack

N_NODES, N_EDGES, D, D_EDGE, D_Q = 3125, 53125, 256, 64, 16
P = 128
TILES = (N_NODES + P - 1) // P
ROWS = TILES * P
STEPS = 416
EDGES = P * STEPS
G = 4
GROUPS = STEPS // G
PAIRS = STEPS // 2
OF_SLOT = [7, 6, 6, 6]
RING = 4
IDX_RING = 8
BIG = 3.0e38
EPS = 1e-5
W_TAB = [D, D, D, D + D_Q, D, 2 * D]
W_STATE = [D, D, D, D + 2, D, D]
MAX, WSUM, SUM, MLP = "max", "weighted sum", "sum", "gated mlp"
KIND = [MAX, MAX, MAX, WSUM, SUM, MLP]
(M_PROJ, M_A_H, M_A_P, M_B_H, M_B_P, M_C_H, M_C_P, M_Q, M_S_H, M_S_P, M_EDGE) = range(11)
POOLED = (M_A_P, M_B_P, M_C_P, M_S_P)
BY_DVE = POOLED + (M_S_H,)
WGT_AT = {M_PROJ: 0, M_A_H: 2, M_A_P: 4, M_B_H: 6, M_B_P: 8, M_C_H: 10, M_C_P: 12, M_S_H: 14, M_S_P: 16}
BIASES = {M_PROJ: [0], M_A_H: [1], M_B_H: [2], M_C_H: [3], M_S_H: [4, 5], M_EDGE: [6, 7]}
B_CORE = 8
STAGE_W = {M_Q: D_Q, M_EDGE: 2 * D}


def build(nc, dram, out):
    f32, i32, bf16, f32r = mybir.dt.float32, mybir.dt.int32, mybir.dt.bfloat16, mybir.dt.float32r
    ALU, ACT, AX = mybir.AluOpType, mybir.ActivationFunctionType, mybir.AxisListType
    ds = bass.ds

    ctx = ExitStack()
    with ctx:
        def sb(name, shape, dt=f32):
            return ctx.enter_context(nc.sbuf_tensor(name, shape, dt))

        def sem(name):
            return ctx.enter_context(nc.semaphore(name))

        X = sb("X", [P, TILES * D])
        H = sb("H", [P, TILES * D])
        PG_W = STEPS * D_Q
        PG = sb("PG", [P, PG_W])
        RING_W = RING * G * 2 * D
        arena = sb("arena", [P, RING_W + 4272])
        state = sb("state", [P, RING * G, D + 2])
        wgt = sb("wgt", [P, 18, D])
        wq = sb("wq", [P, 2, D_Q])
        wedge = sb("wedge", [P, 2, 2 * D])
        wattr_hi = sb("wattr_hi", [P, 2 * D], f32r)
        wattr_lo = sb("wattr_lo", [P, 2 * D], f32r)
        attr_split = sb("attr_split", [P, 2, G * P], f32r)
        bias = sb("bias", [P, 9 * D], f32r)
        bias_rows = sb("bias_rows", [P, P], f32r)
        lnw = sb("lnw", [P, 6, D])
        ident = sb("ident", [P, P])
        ones_sq = sb("ones_sq", [P, P])
        iota_lo = sb("iota_lo", [P, P], bf16)
        iota_hi = sb("iota_hi", [P, TILES], bf16)
        zeros = sb("zeros", [P, D + 2])
        aT = sb("aT", [P, 2, 2, P])
        idx = sb("idx", [P, IDX_RING * G], i32)
        dst_prev = sb("dst_prev", [P, STEPS + 1], i32)
        dsti = dst_prev[:, 1:]
        keep_sum = sb("keep_sum", [P, STEPS])
        keep_max = sb("keep_max", [P, STEPS])
        Q = sb("Q", [P, TILES * D_Q])
        qhead = sb("qhead", [P, D_Q])
        stat = sb("stat", [P, TILES * 6])
        mv = sb("mv", [P, 2, TILES])
        sd = sb("sd", [P, TILES])
        rstd = sb("rstd", [P, TILES])
        nmr = sb("nmr", [P, TILES])
        cnt = sb("cnt", [P, TILES])
        tmp = sb("tmp", [P, 8, 32])
        some = sb("some", [P, TILES])
        end_i = sb("end_i", [P, TILES], i32)
        start_i = sb("start_i", [P, TILES], i32)
        head_i = sb("head_i", [P, 1], i32)
        icnt = sb("icnt", [P, TILES])
        pcol = sb("pcol", [P, 4])
        eps_t = sb("eps_t", [P, 1])
        chain_sum = sb("chain_sum", [P, P])
        chain_max = sb("chain_max", [P, P])
        cont_max = sb("cont_max", [P, 1])
        cont_sum = sb("cont_sum", [P, 1])
        carryT = sb("carryT", [P, 3, P + 1])
        headrow = sb("headrow", [P, D + 2])
        mend = sb("mend", [P, D + 2])
        rn = sb("rn", [P, TILES])

        def slots(at, n, w):
            return arena[:, at:at + n * w].rearrange("p (s w) -> p s w", w=w)

        ring_mlp = slots(0, RING * G, 2 * D)
        ring_wide = slots(0, RING * G, D + D_Q)
        ring_one = slots(0, RING * G, D)
        RINGS = {MAX: ring_one, SUM: ring_one, WSUM: ring_wide, MLP: ring_mlp}
        Y = arena[:, RING * G * D:RING * G * D + TILES * D]
        after = RING * G * D + TILES * D
        tri = arena[:, after:after + P]
        dst_lo = arena[:, after + P:after + P + STEPS // 2].bitcast(bf16)
        dst_hi = arena[:, after + P + STEPS // 2:after + P + STEPS].bitcast(bf16)
        HOT_W = P + 32
        hot = arena[:, after + P + STEPS:after + P + STEPS + RING * G * HOT_W // 2].bitcast(bf16) \
            .rearrange("p (s w) -> p s w", w=HOT_W)
        weighted = slots(RING_W, RING * G, D + 2)
        qprod = slots(RING_W + 4128, 2 * G, D_Q)[:, 0:G, :]
        edot = arena[:, RING_W + 4256:RING_W + 4256 + G]
        hidT = slots(RING_W, 2, 4 * P)
        msg = slots(RING_W + 1024, 2, 2 * D)
        attr_raw = slots(RING_W + 2048, 2, G * P)
        raw_bias = state[:, 0:9, 0:D]
        raw_wattr = state[:, 9:11, 0:D]
        split_tmp = state[:, 11:13, 0:D]
        w2 = wgt[:, 0:2, :]

        tp = [ctx.enter_context(nc.psum_tensor(f"tp{i}", [P, 512], f32)) for i in range(2)]
        mm_pair = ctx.enter_context(nc.psum_tensor("mm_pair", [P, 1024], f32))
        mm = [mm_pair[:, 0:512], mm_pair[:, 512:1024]]
        core = [ctx.enter_context(nc.psum_tensor(f"core{i}", [P, 512], f32)) for i in range(2)]
        tailT = ctx.enter_context(nc.psum_tensor("tailT", [P, 512], f32))
        tailU = ctx.enter_context(nc.psum_tensor("tailU", [P, 512], f32))

        x_in, small_in, dst_in, w_in = sem("x_in"), sem("small_in"), sem("dst_in"), sem("w_in")
        consts = sem("consts")
        zero_out = sem("zero_out")
        masks_done = sem("masks_done")
        prep_step = sem("prep_step")
        idx_in = [sem(f"idx_in{i}") for i in range(IDX_RING)]
        rows_in = [sem(f"rows_in{i}") for i in range(RING)]
        state_done = sem("state_done")
        dumped = [sem(f"dumped{i}") for i in range(RING)]
        hot_done, hot_used = sem("hot_done"), sem("hot_used")
        count_done, rank_done = sem("count_done"), sem("rank_done")
        count_here = sem("count_here")
        positions = sem("positions")
        chain_row, chain_rhs = sem("chain_row"), sem("chain_rhs")
        tail_T, tail_scan, tail_U = sem("tail_T"), sem("tail_scan"), sem("tail_U")
        head_in, head_out, mended = sem("head_in"), sem("head_out"), sem("mended")
        pooled_in = [sem(f"pooled_in{i}") for i in range(4)]
        qslot_out, qhead_in, qedge_in = sem("qslot_out"), sem("qhead_in"), sem("qedge_in")
        qhead_set, qedge_scan = sem("qhead_set"), sem("qedge_scan")
        tp_ready, at_ready, mm_ready, mm_used = (sem(n) for n in ("tp_ready", "at_ready", "mm_ready", "mm_used"))
        out_act, out_dve = sem("out_act"), sem("out_dve")
        stats_done = sem("stats_done")
        node_step = sem("node_step")
        var_ready, sd_ready, norm_ready = sem("var_ready"), sem("sd_ready"), sem("norm_ready")
        h_norm = sem("h_norm")
        tab_out = [sem(f"tab_out{i}") for i in range(5)]
        tab5_out = [sem(f"tab5_out{i}") for i in range(4)]
        bias_set, wattr_set, w2_in = sem("bias_set"), sem("wattr_set"), sem("w2_in")
        relu_done = sem("relu_done")
        beta_added = sem("beta_added")
        attr_hi, attr_done = sem("attr_hi"), sem("attr_done")
        dot_step, dot_done, wrow_done = sem("dot_step"), sem("dot_done"), sem("wrow_done")
        z_ready, z_done, sig_done = sem("z_ready"), sem("z_done"), sem("sig_done")
        hT_ready, hT_done, core_ready, msg_done = (sem(n) for n in ("hT_ready", "hT_done", "core_ready", "msg_done"))
        attr_in = [sem(f"attr_in{i}") for i in range(2)]
        pace = sem("pace")
        y_out = sem("y_out")

        block = ctx.enter_context(nc.Block())

        def col(t, k, w, n=None):
            n = w if n is None else n
            return t[:, k * w:k * w + n] if isinstance(k, int) else t[:, ds(k * w, n)]

        def wait(eng, s, v):
            if not isinstance(v, int) or v > 0:
                eng.wait_ge(s, v)

        def wait_paced(eng, s, v):
            wait(eng, s, v)
            if not isinstance(v, int):
                eng.sem_inc(pace)

        def tiles(eng, body):
            for k in range(4):
                body(k, k)
            with eng.Fori(1, TILES // 4) as r:
                for i in range(4):
                    body(r * 4 + i, i)
            body(TILES - 1, 0)

        def groups(eng, body, unroll):
            for g in range(unroll):
                body(g, g)
            with eng.Fori(1, GROUPS // unroll) as r:
                for i in range(unroll):
                    body(r * unroll + i, i)

        def consumer(m):
            return (mm_used if m in BY_DVE else out_act), TILES * sum((i in BY_DVE) == (m in BY_DVE) for i in range(m))

        Q_BASE, EDGE_BASE = consumer(M_Q)[1], consumer(M_EDGE)[1]

        def earlier(g, slot, h, lag):
            d = (h - lag) // 2
            return g * 2 + (h - lag), g + d, (slot + d) % RING, (h - lag) % 2

        def used_rows(ps, g):
            return (msg_done, g * (G // 2)) if KIND[ps] == MLP else (state_done, ps * STEPS + g * G)

        def state_rows(ps):
            t = dram["states_wide"] if W_STATE[ps] > D else dram["states"]
            return t

        @block.sync
        def _(sp):
            sp.dma_start(X[:, :].rearrange("p (k w) -> p k w", w=D),
                         dram["x"].rearrange("(k p) w -> p k w", p=P)).then_inc(x_in, 16)
            sp.dma_start(dst_prev[:, :], dram["dst"]).then_inc(dst_in, 16)
            for row in (0, 32):
                sp.dma_start(raw_bias[row:row + 1, :, :], dram["bias"]).then_inc(small_in, 16)
            for row in (0, D_EDGE):
                sp.dma_start(raw_wattr[row:row + D_EDGE, :, :], dram["w_attr"]).then_inc(small_in, 16)
            sp.dma_start(wgt[:, 0:2, :], dram["w_proj"]).then_inc(small_in, 16)
            for at, name in ((2, "w_l0a"), (6, "w_l0b"), (10, "w_l0c"), (14, "w_sage")):
                sp.dma_start(wgt[:, at:at + 4, :], dram[name]).then_inc(w_in, 16)
            for t, name in ((wq[:, :, :], "w_q"), (wedge[:, :, :], "w_edge")):
                sp.dma_start(t, dram[name]).then_inc(w_in, 16)
            for i in range(6):
                sp.dma_start(lnw[:, i, :], dram["ln"][i:i + 1, :].to_broadcast([P, D])).then_inc(w_in, 16)
            wait(sp, consts, 1)
            sp.dma_start(dram["states"][EDGES:EDGES + 1, :], zeros[0:1, 0:D]).then_inc(zero_out, 16)
            sp.dma_start(dram["states_wide"][EDGES:EDGES + 1, :], zeros[0:1, :]).then_inc(zero_out, 16)
            for i in range(2 * D_Q):
                half = STEPS // 2 * D_Q // D_Q
                sp.dma_start(dram["q_edge"][0:EDGES, :].rearrange("(p t) w -> p (t w)", t=STEPS)[:, i * half:(i + 1) * half],
                             zeros[:, 0:half]).then_inc(zero_out, 16)

            def table(ps, src, width, s, first, at=0):
                def body(k, slot):
                    wait(sp, s, first + k + 1)
                    rows = dram[f"table{ps}"][k * P:(k + 1) * P, at:at + width] if isinstance(k, int) \
                        else dram[f"table{ps}"][ds(k * P, P), at:at + width]
                    sp.dma_start(rows, col(src, k, width)).then_inc(tab_out[ps], 16)
                tiles(sp, body)

            def spool(ps):
                w = W_STATE[ps]
                rows = state_rows(ps)[0:EDGES, :].rearrange("(p t) w -> p (t w)", t=STEPS)
                per = GROUPS // IDX_RING

                def dump(g, slot):
                    wait(sp, state_done, ps * STEPS + g * G + G)
                    piece = rows[:, g * G * w:(g + 1) * G * w] if isinstance(g, int) else rows[:, ds(g * (G * w), G * w)]
                    sp.dma_start(piece.rearrange("p (t w) -> p t w", w=w),
                                 state[:, slot * G:slot * G + G, 0:w]).then_inc(dumped[slot], 16)

                def load_idx(g, slot):
                    piece = dram["src"][g] if isinstance(g, int) else dram["src"][ds(g, 1)].rearrange("a p k -> (a p) k")
                    sp.dma_start(idx[:, slot * G:slot * G + G], piece).then_inc(idx_in[slot], 16)

                def load_attr(g, slot):
                    piece = dram["attr"][g] if isinstance(g, int) else dram["attr"][ds(g, 1)].rearrange("a p k -> (a p) k")
                    for row in (0, D_EDGE):
                        sp.dma_start(attr_raw[row:row + D_EDGE, slot, :], piece).then_inc(attr_in[slot], 16)

                for g in range(IDX_RING):
                    load_idx(g, g)
                if KIND[ps] == MLP:
                    sp.dma_start(w2, dram["w_2"]).then_inc(w2_in, 16)
                    for g in range(2):
                        load_attr(g, g)
                lag = 2 if KIND[ps] == MLP else 0

                def body(g, slot):
                    if lag and not (isinstance(g, int) and g + 2 >= GROUPS):
                        wait(sp, attr_done, g + 1)
                        load_attr(g + 2, slot % 2)
                    if not isinstance(g, int) or g >= lag:
                        dump(g - lag, (slot - lag) % RING)
                        if not isinstance(g, int) or g - lag + IDX_RING < GROUPS:
                            wait(sp, *used_rows(ps, g - lag + 1))
                            load_idx(g - lag + IDX_RING, (slot - lag) % IDX_RING)
                for g in range(IDX_RING):
                    body(g, g)
                with sp.Fori(1, per - 1) as r:
                    for i in range(IDX_RING):
                        body(r * IDX_RING + i, i)
                for g in range(GROUPS - IDX_RING, GROUPS):
                    body(g, g % IDX_RING)
                for g in range(GROUPS - lag, GROUPS):
                    dump(g, g % RING)

            table(0, PG, D, out_act, 0)
            spool(0)
            table(1, H, D, relu_done, 0)
            spool(1)
            table(2, H, D, out_dve, 0)
            spool(2)
            table(3, H, D, h_norm, 3 * TILES)
            table(3, Q, D_Q, out_act, Q_BASE, at=D)

            def q_table(k, slot):
                rows = dram["q_node"][k * P:(k + 1) * P, :] if isinstance(k, int) else dram["q_node"][ds(k * P, P), :]
                sp.dma_start(rows, col(Q, k, D_Q)).then_inc(tab_out[3], 16)
            tiles(sp, q_table)
            wait(sp, qslot_out, 16 * TILES)
            sp.dma_start(PG[:, :], dram["q_edge"][0:EDGES, :].rearrange("(p t) w -> p (t w)", t=STEPS)).then_inc(qedge_in, 16)
            spool(3)
            table(4, H, D, h_norm, 4 * TILES)
            spool(4)

            def edge_table(k, slot):
                wait(sp, out_act, EDGE_BASE + k + 1)
                rows = dram["table5"][k * P:(k + 1) * P, :] if isinstance(k, int) else dram["table5"][ds(k * P, P), :]
                sp.dma_start(rows, ring_mlp[:, slot, :]).then_inc(tab5_out[slot], 16)
            tiles(sp, edge_table)
            spool(5)

            def result(k, slot):
                wait(sp, out_dve, TILES + k + 1)
                rows = out[k * P:(k + 1) * P, :] if isinstance(k, int) else out[ds(k * P, P), :]
                sp.dma_start(rows, col(X, k, D)).then_inc(y_out, 16)
            for k in range(4):
                result(k, k)
            with sp.Fori(1, TILES // 4) as r:
                for i in range(4):
                    result(r * 4 + i, i)
            last_rows = N_NODES - (TILES - 1) * P
            wait(sp, out_dve, 2 * TILES)
            sp.dma_start(out[(TILES - 1) * P:N_NODES, :], X[0:last_rows, (TILES - 1) * D:]).then_inc(y_out, 16)
            sp.wait_ge(y_out, 16 * TILES)

        @block.gpsimd
        def _(pool):
            pool.memset(zeros[:, :], 0.0).then_inc(consts, 1)
            pool.memset(ones_sq[:, :], 1.0).then_inc(consts, 1)
            pool.memset(ident[:, :], 0.0).then_inc(consts, 1)
            pool.memset(tri, 1.0).then_inc(consts, 1)
            pool.memset(eps_t[:, :], EPS).then_inc(consts, 1)
            pool.memset(carryT[:, :, :], 0.0).then_inc(consts, 1)
            pool.iota(iota_lo[:, :], [[1, P]], base=0, channel_multiplier=0,
                      allow_small_or_imprecise_dtypes=True).then_inc(consts, 1)
            pool.iota(iota_hi[:, :], [[1, TILES]], base=0, channel_multiplier=0,
                      allow_small_or_imprecise_dtypes=True).then_inc(consts, 1)
            pool.iota(rn[:, :], [[P, TILES]], base=0, channel_multiplier=1,
                      allow_small_or_imprecise_dtypes=True).then_inc(consts, 1)
            pool.iota(pcol[:, 0:1], [[1, 1]], base=0, channel_multiplier=STEPS,
                      allow_small_or_imprecise_dtypes=True).then_inc(consts, 1)
            pool.memset(bias[:, :].bitcast(f32), 0.0).then_inc(consts, 1)
            pool.memset(bias_rows[:, :].bitcast(f32), 0.0).then_inc(consts, 1)
            pool.wait_ge(consts, 12)
            pool.affine_select(out=ident[:, :], in_=ident[:, :], compare_op=ALU.not_equal, fill=1.0,
                               base=0, pattern=[[-1, P]], channel_multiplier=1).then_inc(consts, 1)
            pool.affine_select(out=tri, in_=tri, compare_op=ALU.is_ge, fill=0.0,
                               base=0, pattern=[[1, P]], channel_multiplier=-1).then_inc(consts, 1)

            def run_pass(ps):
                w = W_TAB[ps]
                count = 75 if ps == 3 else 25
                if ps == 5:
                    for slot, s in enumerate(tab5_out):
                        pool.wait_ge(s, 16 * OF_SLOT[slot])
                else:
                    pool.wait_ge(tab_out[ps], 16 * count)
                per = GROUPS // IDX_RING

                def body(g, slot):
                    base = (ps * per + 1) * 16
                    wait_paced(pool, idx_in[slot], base if isinstance(g, int) else (g // IDX_RING) * 16 + base)
                    if not (isinstance(g, int) and g < RING):
                        wait_paced(pool, *used_rows(ps, g - (RING - 1)))
                    rs = slot % RING
                    for i in range(G):
                        pool.indirect_dma_start(RINGS[KIND[ps]][:, rs * G + i, 0:w], None, dram[f"table{ps}"],
                                                bass.IndirectOffsetOnAxis(idx[:, slot * G + i:slot * G + i + 1], 0)
                                                ).then_inc(rows_in[rs], 16)
                groups(pool, body, IDX_RING)

            def finish_pass(ps):
                w = W_STATE[ps]
                t = state_rows(ps)
                for s in dumped:
                    s_per = GROUPS // RING
                    pool.wait_ge(s, 16 * s_per * (ps + 1))
                if ps == 0:
                    pool.wait_ge(positions, 2)
                pool.indirect_dma_start(headrow[:, 0:w], None, t, bass.IndirectOffsetOnAxis(head_i[:, 0:1], 0)).then_inc(head_in, 16)
                pool.wait_ge(mended, ps + 1)
                pool.indirect_dma_start(t, bass.IndirectOffsetOnAxis(head_i[:, 0:1], 0), mend[:, 0:w], None).then_inc(head_out, 16)
                pool.wait_ge(head_out, 16 * (ps + 1))
                if ps == 0:
                    pool.wait_ge(zero_out, 16 * (2 + 2 * D_Q))
                for k in range(TILES):
                    i, r = k % 4, k // 4
                    before = 16 * (ps * OF_SLOT[i] + r)
                    if before:
                        pool.wait_ge(pooled_in[i], before)
                    pool.indirect_dma_start(PG[:, k * w:k * w + w], None, t,
                                            bass.IndirectOffsetOnAxis(end_i[:, k:k + 1], 0)).then_inc(pooled_in[i], 16)

            for ps in range(6):
                if ps == 3:
                    for k in range(TILES):
                        pool.wait_ge(out_act, Q_BASE + k + 1)
                        pool.indirect_dma_start(dram["q_edge"], bass.IndirectOffsetOnAxis(start_i[:, k:k + 1], 0),
                                                Q[:, k * D_Q:(k + 1) * D_Q], None).then_inc(qslot_out, 16)
                    pool.wait_ge(tab_out[3], 16 * 75)
                    pool.indirect_dma_start(qhead[:, :], None, dram["q_node"],
                                            bass.IndirectOffsetOnAxis(dst_prev[:, 1:2], 0)).then_inc(qhead_in, 16)
                if ps == 5:
                    def add_beta(k, slot):
                        wait_paced(pool, h_norm, 5 * TILES + k + 1)
                        x = col(X, k, D)
                        pool.tensor_tensor(x, x, lnw[:, 5, :], ALU.add).then_inc(beta_added, 1)
                    tiles(pool, add_beta)
                run_pass(ps)
                finish_pass(ps)

        @block.tensor
        def _(pe):
            def stage(m, ready):
                w, base = STAGE_W.get(m, D), m * TILES
                used, used_base = consumer(m)
                src = PG if m in POOLED else H

                def transposes(k, slot):
                    ready(k, slot)
                    wait(pe, at_ready, base + max(k - 1, 0))
                    for c in range(2):
                        last = nc.tensor.transpose(tp[slot % 2][:, c * P:(c + 1) * P],
                                                   src[:, k * D + c * P:k * D + c * P + P], ident[:, :])
                    last.then_inc(tp_ready, 1)

                def multiply(k, slot):
                    wait(pe, at_ready, base + k + 1)
                    if k == 0 and m > 0:
                        before, before_base = consumer(m - 1)
                        wait(pe, before, before_base + TILES)
                    wait(pe, used, used_base + max(k - 1, 0))
                    o = mm[slot % 2][:, 0:w]
                    rows = BIASES.get(m, [])
                    for c in range(2):
                        rhs = wq[:, c, :] if m == M_Q else wedge[:, c, :] if m == M_EDGE else wgt[:, WGT_AT[m] + c, :]
                        last = nc.tensor.matmul(o, aT[:, slot % 2, c, :], rhs, start=(c == 0), stop=(c == 1 and not rows))
                    if m == M_EDGE:
                        last = nc.tensor.matmul(o, bias_rows[:, :], bias[:, rows[0] * D:(rows[-1] + 1) * D], start=False, stop=True)
                    else:
                        for n, b in enumerate(rows):
                            last = nc.tensor.matmul(o, bias_rows[:, :], bias[:, b * D:(b + 1) * D], start=False,
                                                    stop=(n == len(rows) - 1))
                    last.then_inc(mm_ready, 1)

                for k in range(TILES):
                    transposes(k, k % 4)
                    if k:
                        multiply(k - 1, (k - 1) % 4)
                multiply(TILES - 1, 0)

            def nothing(k, slot):
                pass

            def pooled(ps):
                def ready(k, slot):
                    n = OF_SLOT[slot]
                    wait(pe, pooled_in[slot], (k // 4) * 16 + 16 * (ps * n + 1))
                return ready

            def counts():
                o = tailU[:, 0:TILES]
                nc.tensor.matmul(o, ones_sq[:, :], zeros[:, 0:TILES], start=True, stop=False)

                def body(g, slot):
                    wait(pe, hot_done, g * G + G)
                    for i in range(G):
                        row = hot[:, slot * G + i, :]
                        last = nc.tensor.matmul(o, row[:, 0:P], row[:, P:P + TILES], start=False, stop=False)
                    last.then_inc(hot_used, 1)
                groups(pe, body, RING)
                nc.tensor.matmul(o, ones_sq[:, :], zeros[:, 0:TILES], start=False, stop=True).then_inc(count_done, 1)
                pe.wait_ge(count_here, 1)
                nc.tensor.matmul(tailU[:, 64:64 + TILES], tri, cnt[:, :], start=True, stop=True)
                nc.tensor.matmul(tailU[:, 128:128 + TILES], ones_sq[:, :], cnt[:, :], start=True, stop=True).then_inc(rank_done, 1)
                pe.wait_ge(chain_rhs, 1)
                pe.wait_ge(positions, 1)
                nc.tensor.matmul(tailU[:, 256:384], ones_sq[:, :], chain_sum[:, :], start=True, stop=True).then_inc(chain_row, 1)

            def tail(ps):
                w = W_STATE[ps]
                pe.wait_ge(state_done, STEPS * (ps + 1))
                if ps == 0:
                    pe.wait_ge(positions, 2)
                blocks = [(0, P), (P, P)] + ([(2 * P, 2)] if w > D else [])
                for b, (at, n) in enumerate(blocks):
                    last = nc.tensor.transpose(tailT[0:n, b * P:(b + 1) * P], state[:, RING * G - 1, at:at + n], ident[:, :])
                last.then_inc(tail_T, 1)
                pe.wait_ge(tail_scan, 3 * ps + 3)
                for b, (at, n) in enumerate(blocks):
                    last = nc.tensor.transpose(tailU[:, at:at + n], carryT[0:n, b, 0:P], ident[0:n, 0:n])
                last.then_inc(tail_U, 1)

            def edge_mlp():
                pe.wait_ge(out_act, EDGE_BASE + TILES)
                pe.wait_ge(w2_in, 16)

                def attr_part(u, g, slot, h):
                    if h == 0:
                        wait(pe, attr_done, g + 1)
                    wait(pe, z_done, u)
                    for i in range(2):
                        rows = attr_split[:, slot % 2, (2 * h + i) * P:(2 * h + i + 1) * P]
                        nc.tensor.matmul(mm[i], rows, wattr_hi[:, :], start=True, stop=False)
                        last = nc.tensor.matmul(mm[i], rows, wattr_lo[:, :], start=False, stop=True)
                    last.then_inc(z_ready, 1)

                def hidden_T(u, slot, h):
                    wait(pe, z_done, u + 1)
                    wait(pe, hT_done, u - 1)
                    for i in range(2):
                        for c in range(2):
                            last = nc.tensor.transpose(tp[h][:, (2 * i + c) * P:(2 * i + c + 1) * P],
                                                       ring_mlp[:, slot * G + 2 * h + i, c * P:(c + 1) * P], ident[:, :])
                    last.then_inc(hT_ready, 1)

                def core_part(u, slot, h):
                    wait(pe, hT_done, u + 1)
                    wait(pe, msg_done, u - 1)
                    for i in range(2):
                        o = core[h][:, i * D:(i + 1) * D]
                        for c in range(2):
                            nc.tensor.matmul(o, hidT[:, h, (2 * i + c) * P:(2 * i + c + 1) * P], w2[:, c, :], start=(c == 0), stop=False)
                        last = nc.tensor.matmul(o, bias_rows[:, :], bias[:, B_CORE * D:(B_CORE + 1) * D], start=False, stop=True)
                    last.then_inc(core_ready, 1)

                def body(g, slot):
                    for h in range(2):
                        attr_part(g * 2 + h, g, slot, h)
                        for lag, part in ((1, hidden_T), (2, core_part)):
                            u, _, s, hh = earlier(g, slot, h, lag)
                            if not isinstance(u, int) or u >= 0:
                                part(u, s, hh)
                groups(pe, body, RING)
                hidden_T(PAIRS - 1, RING - 1, 1)
                core_part(PAIRS - 2, RING - 1, 0)
                core_part(PAIRS - 1, RING - 1, 1)

            pe.wait_ge(consts, 14)
            pe.wait_ge(bias_set, 3)
            stage(M_PROJ, lambda k, slot: wait(pe, h_norm, k + 1))
            pe.wait_ge(w_in, 16 * 12)
            stage(M_A_H, nothing)
            counts()
            tail(0)
            stage(M_A_P, pooled(0))
            stage(M_B_H, lambda k, slot: wait(pe, relu_done, k + 1))
            tail(1)
            stage(M_B_P, pooled(1))
            stage(M_C_H, lambda k, slot: wait(pe, out_dve, k + 1))
            tail(2)
            stage(M_C_P, pooled(2))
            stage(M_Q, lambda k, slot: wait(pe, h_norm, 3 * TILES + k + 1))
            tail(3)
            stage(M_S_H, lambda k, slot: wait(pe, h_norm, 4 * TILES + k + 1))
            tail(4)
            stage(M_S_P, pooled(4))
            stage(M_EDGE, lambda k, slot: wait(pe, h_norm, 5 * TILES + k + 1))
            pe.wait_ge(wattr_set, 2)
            edge_mlp()
            tail(5)

        @block.scalar
        def _(act):
            def stage(m, output):
                base = m * TILES

                def copy_T(k, slot):
                    wait(act, tp_ready, base + k + 1)
                    if isinstance(k, int):
                        wait(act, mm_ready, base + max(k - 1, 0))
                    else:
                        wait(act, mm_ready, base + k - 1)
                    nc.scalar.activation(aT[:, slot % 2, :, :], tp[slot % 2][:, 0:2 * P].rearrange("p (c n) -> p c n", n=P),
                                         ACT.Copy).then_inc(at_ready, 1)

                def body(k, slot):
                    copy_T(k, slot)
                    if output and not (isinstance(k, int) and k == 0):
                        output(k - 1, (slot - 1) % 4)
                tiles(act, body)
                if output:
                    output(TILES - 1, 0)

            def root(n):
                act.wait_ge(var_ready, n)
                nc.scalar.activation(sd[:, :], mv[:, 1, :], ACT.Sqrt, bias=eps_t[:, 0:1]).then_inc(sd_ready, 1)

            def normalise(n, func, src, dst):
                act.wait_ge(norm_ready, n)

                def body(k, slot):
                    rs = rstd[:, k:k + 1] if isinstance(k, int) else rstd[:, ds(k, 1)]
                    nm = nmr[:, k:k + 1] if isinstance(k, int) else nmr[:, ds(k, 1)]
                    nc.scalar.activation(col(dst, k, D), col(src, k, D), func, bias=nm, scale=rs).then_inc(h_norm, 1)
                tiles(act, body)

            def product_to(m, dst, func):
                def output(k, slot):
                    wait(act, mm_ready, m * TILES + k + 1)
                    nc.scalar.activation(col(dst, k, D), mm[slot % 2][:, 0:D], func).then_inc(out_act, 1)
                return output

            def relu_y(k, slot):
                wait(act, mm_used, consumer(M_A_P)[1] + k + 1)
                nc.scalar.activation(col(H, k, D), col(Y, k, D), ACT.Relu).then_inc(relu_done, 1)

            def weigh_rows():
                def body(g, slot):
                    wait(act, dot_done, g + 1)
                    wait(act, state_done, 3 * STEPS + (g - (RING - 1)) * G if not isinstance(g, int) else (3 * STEPS + (g - (RING - 1)) * G if g >= RING else 0))
                    for i in range(G):
                        s = slot * G + i
                        last = nc.scalar.activation(weighted[:, s, 0:D], ring_wide[:, s, 0:D], ACT.Copy,
                                                    scale=weighted[:, s, D:D + 1])
                        last.then_inc(wrow_done, 1)
                groups(act, body, RING)

            def edge_gates():
                def attr_high(g, slot):
                    wait(act, attr_in[slot % 2], g // 2 * 32 + 32)
                    wait(act, z_ready, g * 2 - 2)
                    nc.scalar.activation(attr_split[:, slot % 2, :], attr_raw[:, slot % 2, :], ACT.Copy).then_inc(attr_hi, 1)

                def gate(u, slot, h):
                    wait(act, z_done, u + 1)
                    z = ring_mlp[:, slot * G + 2 * h:slot * G + 2 * h + 2, D:2 * D]
                    nc.scalar.activation(z, z, ACT.Sigmoid).then_inc(sig_done, 1)

                def hidden(u, slot, h):
                    wait(act, hT_ready, u + 1)
                    wait(act, core_ready, u - 1)
                    nc.scalar.activation(hidT[:, h, :], tp[h][:, :], ACT.Relu).then_inc(hT_done, 1)

                def body(g, slot):
                    attr_high(g, slot)
                    for h in range(2):
                        u, _, s, hh = earlier(g, slot, h, 1)
                        if not isinstance(u, int) or u >= 0:
                            gate(u, s, hh)
                            hidden(u, s, hh)
                groups(act, body, RING)
                gate(PAIRS - 1, RING - 1, 1)
                hidden(PAIRS - 1, RING - 1, 1)

            act.wait_ge(consts, 14)
            for row in (0, 32):
                nc.scalar.activation(bias_rows[row:row + 1, :], ones_sq[row:row + 1, :], ACT.Copy).then_inc(bias_set, 1)
            root(1)
            normalise(1, ACT.Relu, X, H)
            stage(M_PROJ, product_to(M_PROJ, PG, ACT.Relu))
            stage(M_A_H, product_to(M_A_H, Y, ACT.Copy))
            stage(M_A_P, relu_y)
            stage(M_B_H, product_to(M_B_H, Y, ACT.Copy))
            stage(M_B_P, None)
            root(2)
            normalise(2, ACT.Identity, H, H)
            stage(M_C_H, product_to(M_C_H, Y, ACT.Copy))
            stage(M_C_P, None)
            root(3)
            normalise(3, ACT.Identity, H, H)
            root(4)
            normalise(4, ACT.Relu, X, H)

            def scaled_q(k, slot):
                wait(act, mm_ready, M_Q * TILES + k + 1)
                nc.scalar.activation(col(Q, k, D_Q), mm[slot % 2][:, 0:D_Q], ACT.Copy, scale=0.25).then_inc(out_act, 1)
            stage(M_Q, scaled_q)
            weigh_rows()
            root(5)
            normalise(5, ACT.Relu, X, H)
            stage(M_S_H, None)
            stage(M_S_P, None)
            root(6)
            normalise(6, ACT.Relu, X, H)

            def staged(k, slot):
                wait(act, mm_ready, M_EDGE * TILES + k + 1)
                if not (isinstance(k, int) and k < 4):
                    wait(act, tab5_out[slot], (k // 4) * 16)
                nc.scalar.activation(ring_mlp[:, slot, :], mm[slot % 2][:, :], ACT.Copy).then_inc(out_act, 1)
            stage(M_EDGE, staged)
            edge_gates()
            root(7)
            normalise(7, ACT.Identity, H, H)

        @block.vector
        def _(dve):
            v = nc.vector
            steps = [0]

            def prep(ins):
                steps[0] += 1
                ins.then_inc(prep_step, 1)
                dve.wait_ge(prep_step, steps[0])

            at = {"base": 0, "n": 0}

            def chained(ins, wait=wait):
                at["n"] += 1
                ins.then_inc(node_step, 1)
                wait(dve, node_step, at["base"] + at["n"])

            def chained_tiles(per, body):
                base = at["base"]

                def one(k, slot):
                    at["base"], at["n"] = base + k * per, 0
                    body(k, slot)
                    assert at["n"] == per
                tiles(dve, one)
                at["base"], at["n"] = base + TILES * per, 0

            def chained_once(ins):
                chained(ins)
                at["base"], at["n"] = at["base"] + 1, 0

            def moments(src, w, k):
                v.bn_stats(col(stat, k, 6), col(src, k, w, D)).then_inc(stats_done, 1)

            norms = [0]

            def invert():
                norms[0] += 1
                dve.wait_ge(stats_done, TILES * norms[0])
                s3 = stat[:, :].rearrange("p (k c) -> p k c", c=6)
                mean_e, dev_e, mean_o, dev_o = (s3[:, :, c] for c in (1, 2, 4, 5))
                v.tensor_tensor(mv[:, 0, :], mean_e, mean_o, ALU.add).then_inc(node_step, 1)
                v.tensor_tensor(mv[:, 1, :], dev_e, dev_o, ALU.add).then_inc(node_step, 1)
                at["base"] += 2
                chained_once(v.tensor_tensor(sd[:, :], mean_e, mean_o, ALU.subtract))
                chained_once(v.tensor_tensor(sd[:, :], sd[:, :], sd[:, :], ALU.mult))
                chained_once(v.tensor_scalar(sd[:, :], sd[:, :], 0.25, None, ALU.mult))
                chained_once(v.scalar_tensor_tensor(out=mv[:, 1, :], in0=mv[:, 1, :], scalar=1.0 / D, in1=sd[:, :],
                                                    op0=ALU.mult, op1=ALU.add))
                v.engine_nop().then_inc(var_ready, 1)
                dve.wait_ge(sd_ready, norms[0])
                chained_once(v.reciprocal(rstd[:, :], sd[:, :]))
                v.scalar_tensor_tensor(out=nmr[:, :], in0=mv[:, 0, :], scalar=-0.5, in1=rstd[:, :],
                                       op0=ALU.mult, op1=ALU.mult).then_inc(norm_ready, 1)
                dve.wait_ge(norm_ready, norms[0])

            def per_tile(t, k):
                return t[:, k:k + 1] if isinstance(k, int) else t[:, ds(k, 1)]

            dve.wait_ge(dst_in, 16)
            dve.wait_ge(consts, 14)
            prep(v.memset(keep_sum[:, 0:1], 0.0))
            prep(v.tensor_tensor(keep_sum[:, 1:], dsti[:, 1:], dsti[:, 0:STEPS - 1], ALU.is_equal))
            v.tensor_scalar(keep_max[:, :], keep_sum[:, :], -1.0, BIG, ALU.add, ALU.mult).then_inc(masks_done, 1)
            dve.wait_ge(masks_done, 1)

            dve.wait_ge(small_in, 16 * 5)
            b3 = bias[:, :].rearrange("p (b w) -> p b w", w=D)
            v.tensor_copy(b3[0:1, :, :], raw_bias[0:1, :, :]).then_inc(bias_set, 1)
            prep(v.tensor_copy(b3[32:33, :, :], raw_bias[32:33, :, :]))
            v.tensor_tensor(b3[32:33, :, :], raw_bias[32:33, :, :], b3[32:33, :, :].bitcast(f32), ALU.subtract)
            hi3, lo3 = (t[:, :].rearrange("p (b w) -> p b w", w=D) for t in (wattr_hi, wattr_lo))
            v.tensor_copy(hi3, raw_wattr).then_inc(wattr_set, 1)
            dve.wait_ge(wattr_set, 1)
            v.tensor_tensor(lo3, raw_wattr, hi3.bitcast(f32), ALU.subtract).then_inc(wattr_set, 1)

            dve.wait_ge(x_in, 16)
            chained_tiles(0, lambda k, slot: moments(X, D, k))
            invert()

            flat = state[:, :, :].rearrange("p s w -> p (s w)")
            lo_i = flat[:, 0:STEPS].bitcast(i32)
            hi_i = flat[:, 512:512 + STEPS].bitcast(i32)
            eq = flat[:, 1024:1024 + STEPS]
            prep(v.tensor_scalar(lo_i, dsti, P - 1, None, ALU.bitwise_and))
            prep(v.tensor_scalar(hi_i, dsti, 7, None, ALU.logical_shift_right))
            prep(v.tensor_copy(dst_lo, lo_i))
            prep(v.tensor_copy(dst_hi, hi_i))
            prep(v.tensor_copy(pcol[:, 1:2], dsti[:, 0:1]))
            prep(v.tensor_tensor(cont_sum[:, :], dsti[:, 0:1], dst_prev[:, 0:1], ALU.is_equal))
            prep(v.tensor_scalar(cont_max[:, :], cont_sum[:, :], -1.0, BIG, ALU.add, ALU.mult))
            prep(v.tensor_copy(eq, dsti))
            prep(v.tensor_scalar(eq, eq, pcol[:, 1:2], None, ALU.is_equal))
            prep(v.tensor_reduce(pcol[:, 3:4], eq, AX.X, ALU.add))
            prep(v.scalar_tensor_tensor(out=tmp[:, 0, 0:1], in0=pcol[:, 3:4], scalar=-1.0, in1=pcol[:, 0:1],
                                        op0=ALU.add, op1=ALU.add))
            prep(v.tensor_copy(head_i[:, :], tmp[:, 0, 0:1]))
            prep(v.scalar_tensor_tensor(out=tmp[:, 1, 0:1], in0=pcol[:, 3:4], scalar=float(STEPS), in1=cont_sum[:, :],
                                        op0=ALU.is_equal, op1=ALU.mult))
            v.tensor_scalar(chain_sum[:, :], ident[:, :], tmp[:, 1, 0:1], None, ALU.mult).then_inc(chain_rhs, 1)

            def scan_step(ps, t, slot, t_mask, src):
                w = W_STATE[ps]
                if isinstance(t, int) and t == 0:
                    v.tensor_copy(state[:, slot, 0:w], src).then_inc(state_done, 1)
                    return
                wait(dve, state_done, ps * STEPS + t)
                mask, op0, op1 = (keep_max, ALU.add, ALU.max) if KIND[ps] == MAX else (keep_sum, ALU.mult, ALU.add)
                v.scalar_tensor_tensor(out=state[:, slot, 0:w], in0=state[:, (slot - 1) % (RING * G), 0:w],
                                       scalar=per_tile(mask, t_mask), in1=src, op0=op0, op1=op1).then_inc(state_done, 1)

            def slot_free(ps, g, slot):
                wait(dve, dumped[slot], (ps * (GROUPS // RING) + g // RING) * 16)

            def rows_there(ps, g, slot):
                wait(dve, rows_in[slot], (ps * (GROUPS // RING) + g // RING + 1) * (16 * G))

            def scan_pass(ps):
                w = W_STATE[ps]

                def body(g, slot):
                    if ps == 0:
                        wait(dve, hot_used, g - (RING - 1) if not isinstance(g, int) else max(g - (RING - 1), 0))
                        for i in range(G):
                            row = hot[:, slot * G + i, :]
                            v.tensor_scalar(row[:, 0:P], iota_lo[:, :], per_tile(dst_lo, g * G + i), None, ALU.is_equal)
                            v.tensor_scalar(row[:, P:P + TILES], iota_hi[:, :], per_tile(dst_hi, g * G + i), None,
                                            ALU.is_equal).then_inc(hot_done, 1)
                    rows_there(ps, g, slot)
                    slot_free(ps, g, slot)
                    for i in range(G):
                        scan_step(ps, g * G + i, slot * G + i, g * G + i, RINGS[KIND[ps]][:, slot * G + i, 0:w])
                groups(dve, body, RING)

            def weighted_pass():
                ps = 3

                def dots(g, slot):
                    rows_there(ps, g, slot)
                    if not (isinstance(g, int) and g < RING):
                        wait(dve, state_done, ps * STEPS + (g - RING + 1) * G)
                    n = g * 3
                    rs = slice(slot * G, slot * G + G)
                    qd = PG[:, g * G * D_Q:(g + 1) * G * D_Q] if isinstance(g, int) else PG[:, ds(g * (G * D_Q), G * D_Q)]
                    v.tensor_tensor(qprod, ring_wide[:, rs, D:D + D_Q], qd.rearrange("p (t w) -> p t w", w=D_Q),
                                    ALU.mult).then_inc(dot_step, 1)
                    wait(dve, dot_step, n + 1)
                    v.tensor_reduce(edot, qprod, AX.X, ALU.add).then_inc(dot_step, 1)
                    wait(dve, dot_step, n + 2)
                    v.tensor_scalar(weighted[:, rs, D + 1], edot, -1.0, 0.0, ALU.mult, ALU.max).then_inc(dot_step, 1)
                    wait(dve, dot_step, n + 3)
                    v.tensor_scalar(weighted[:, rs, D], edot, 0.0, None, ALU.max).then_inc(dot_done, 1)

                def scans(g, slot):
                    slot_free(ps, g, slot)
                    for i in range(G):
                        wait(dve, wrow_done, g * G + i + 1)
                        scan_step(ps, g * G + i, slot * G + i, g * G + i, weighted[:, slot * G + i, :])

                def body(g, slot):
                    dots(g, slot)
                    if not (isinstance(g, int) and g == 0):
                        scans(g - 1, (slot - 1) % RING)
                groups(dve, body, RING)
                scans(GROUPS - 1, RING - 1)

            def mlp_pass():
                ps = 5
                dve.wait_ge(out_act, EDGE_BASE + TILES)

                def attr_low(g, slot):
                    wait(dve, attr_hi, g + 1)
                    low = attr_split[D_EDGE:P, slot % 2, :]
                    v.tensor_tensor(low, attr_raw[D_EDGE:P, slot % 2, :], low.bitcast(f32), ALU.subtract).then_inc(attr_done, 1)

                def add(u, g, slot, h):
                    if h == 0:
                        rows_there(ps, g, slot)
                    wait(dve, z_ready, u + 1)
                    z = ring_mlp[:, slot * G + 2 * h:slot * G + 2 * h + 2, :]
                    v.tensor_tensor(z, mm_pair[:, :].rearrange("p (s w) -> p s w", w=2 * D), z, ALU.add).then_inc(z_done, 1)

                def message(u, g, slot, h):
                    s = slot * G + 2 * h
                    wait(dve, core_ready, u + 1)
                    wait(dve, sig_done, u + 1)
                    v.tensor_tensor(msg[:, h, :].rearrange("p (s w) -> p s w", w=D), core[h][:, :].rearrange("p (s w) -> p s w", w=D),
                                    ring_mlp[:, s:s + 2, D:2 * D], ALU.mult).then_inc(msg_done, 1)

                def scan(u, g, slot, h, i):
                    if h == 0 and i == 0:
                        slot_free(ps, g, slot)
                    if i == 0:
                        wait(dve, msg_done, u + 1)
                    scan_step(ps, u * 2 + i, slot * G + 2 * h + i, u * 2 + i, msg[:, h, i * D:(i + 1) * D])

                def turn(g, slot, h, first=0, last=4):
                    back = {lag: earlier(g, slot, h, lag) for lag in (1, 3, 4)}
                    exists = {lag: (not isinstance(b[0], int) or b[0] >= 0) and first <= lag <= last
                              for lag, b in back.items()}
                    if exists[1]:
                        add(*back[1])
                    if exists[4]:
                        scan(*back[4], 0)
                    if exists[3]:
                        message(*back[3])
                    if exists[4]:
                        scan(*back[4], 1)

                def body(g, slot):
                    attr_low(g, slot)
                    for h in range(2):
                        turn(g, slot, h)
                groups(dve, body, RING)
                turn(GROUPS, 0, 0)
                turn(GROUPS, 0, 1, first=2)
                turn(GROUPS + 1, 1, 0, first=2)
                turn(GROUPS + 1, 1, 1, first=4)

            def tail(ps):
                w = W_STATE[ps]
                wide = w > D
                row = chain_max if KIND[ps] == MAX else chain_sum
                op0, op1 = (ALU.add, ALU.max) if KIND[ps] == MAX else (ALU.mult, ALU.add)
                dve.wait_ge(tail_T, ps + 1)
                for b in range(3):
                    n = P if b < 2 else 2
                    if b == 2 and not wide:
                        v.engine_nop().then_inc(tail_scan, 1)
                        continue
                    v.tensor_tensor_scan(carryT[0:n, b, 1:P + 1], row[0:n, :], tailT[0:n, b * P:(b + 1) * P], 0.0,
                                         op0, op1).then_inc(tail_scan, 1)
                dve.wait_ge(tail_U, ps + 1)
                dve.wait_ge(head_in, 16 * (ps + 1))
                if ps:
                    dve.wait_ge(head_out, 16 * ps)
                cont = cont_max if KIND[ps] == MAX else cont_sum
                v.scalar_tensor_tensor(out=mend[:, 0:w], in0=tailU[:, 0:w], scalar=cont[:, 0:1], in1=headrow[:, 0:w],
                                       op0=op0, op1=op1).then_inc(mended, 1)

            def pooled(ps, k, slot):
                n = OF_SLOT[slot]
                wait(dve, pooled_in[slot], (k // 4) * 16 + 16 * (ps * n + 1))

            def product(m, k):
                wait(dve, mm_ready, m * TILES + k + 1)

            dve.wait_ge(prep_step, steps[0])
            scan_pass(0)
            dve.wait_ge(count_done, 1)
            v.tensor_copy(cnt[:, :], tailU[:, 0:TILES]).then_inc(count_here, 1)
            dve.wait_ge(rank_done, 1)
            total, within = tmp[:, 2, 0:TILES], tmp[:, 3, 0:TILES]
            prep(v.tensor_copy(total, tailU[:, 128:128 + TILES]))
            prep(v.tensor_copy(within, tailU[:, 64:64 + TILES]))
            prep(v.tensor_tensor_scan(tmp[:, 4, 0:TILES], ones_sq[:, 0:TILES], total, 0.0, ALU.mult, ALU.add))
            prep(v.tensor_tensor(tmp[:, 4, 0:TILES], tmp[:, 4, 0:TILES], total, ALU.subtract))
            prep(v.tensor_tensor(within, within, tmp[:, 4, 0:TILES], ALU.add))
            prep(v.tensor_scalar(some[:, :], cnt[:, :], 1.0, None, ALU.min))
            prep(v.tensor_scalar(tmp[:, 5, 0:TILES], within, float(-1 - EDGES), None, ALU.add))
            prep(v.tensor_tensor(tmp[:, 5, 0:TILES], tmp[:, 5, 0:TILES], some[:, :], ALU.mult))
            prep(v.tensor_scalar(tmp[:, 5, 0:TILES], tmp[:, 5, 0:TILES], float(EDGES), None, ALU.add))
            prep(v.tensor_copy(end_i[:, :], tmp[:, 5, 0:TILES]))
            prep(v.tensor_tensor(within, within, cnt[:, :], ALU.subtract))
            prep(v.tensor_scalar(rn[:, :], rn[:, :], float(EDGES), None, ALU.add))
            prep(v.tensor_tensor(within, within, rn[:, :], ALU.subtract))
            prep(v.tensor_tensor(within, within, some[:, :], ALU.mult))
            prep(v.tensor_tensor(within, within, rn[:, :], ALU.add))
            prep(v.tensor_copy(start_i[:, :], within))
            prep(v.tensor_scalar(icnt[:, :], cnt[:, :], 1.0, None, ALU.max))
            prep(v.reciprocal(icnt[:, :], icnt[:, :]))
            v.engine_nop().then_inc(positions, 1)
            dve.wait_ge(chain_row, 1)
            prep(v.tensor_copy(chain_sum[:, :], tailU[:, 256:384]))
            prep(v.tensor_scalar(chain_max[:, :], chain_sum[:, :], -1.0, BIG, ALU.add, ALU.mult))
            v.engine_nop().then_inc(positions, 1)
            tail(0)

            def halves(m):
                def add(k, slot):
                    product(m, k)
                    y = col(Y, k, D)
                    v.tensor_tensor(y, mm[slot % 2][:, 0:D], y, ALU.add).then_inc(mm_used, 1)
                    wait(dve, mm_used, consumer(m)[1] + k + 1)
                return add

            def add_relu(m):
                add = halves(m)

                def body(k, slot):
                    add(k, slot)
                    chained(v.scalar_tensor_tensor(out=col(H, k, D), in0=col(Y, k, D), scalar=0.0, in1=col(H, k, D),
                                                   op0=ALU.max, op1=ALU.add))
                    moments(H, D, k)
                chained_tiles(1, body)

            def first(k, slot):
                product(M_A_P, k)
                y = col(Y, k, D)
                v.tensor_tensor(y, mm[slot % 2][:, 0:D], y, ALU.add).then_inc(mm_used, 1)
            tiles(dve, first)
            scan_pass(1)
            tail(1)

            dve.wait_ge(w_in, 16 * 12)
            add_relu(M_B_P)
            invert()

            def second(k, slot):
                h = col(H, k, D)
                wait(dve, h_norm, TILES + k + 1)
                chained(v.tensor_tensor(h, h, lnw[:, 0, :], ALU.mult))
                v.tensor_tensor(h, h, lnw[:, 1, :], ALU.add).then_inc(out_dve, 1)
            chained_tiles(1, second)

            def shift(k, slot):
                chained(v.tensor_tensor(col(X, k, D), col(X, k, D), lnw[:, 3, :], ALU.add))
            chained_tiles(1, shift)
            scan_pass(2)
            tail(2)

            add_relu(M_C_P)
            invert()

            def third(k, slot):
                h, x = col(H, k, D), col(X, k, D)
                wait(dve, h_norm, 2 * TILES + k + 1)
                chained(v.tensor_tensor(h, h, lnw[:, 2, :], ALU.mult))
                chained(v.tensor_tensor(x, x, h, ALU.add))
                moments(X, D, k)
            chained_tiles(2, third)
            invert()

            qe = PG[:, :].rearrange("p (t w) -> p t w", w=D_Q)
            dve.wait_ge(qedge_in, 16)
            dve.wait_ge(qhead_in, 16)
            prep(v.tensor_copy(qe[:, 0, :], qhead[:, :]))
            for c in range(D_Q):
                prep(v.tensor_tensor_scan(qe[:, :, c], keep_sum[:, :], qe[:, :, c], 0.0, ALU.mult, ALU.add))
            weighted_pass()
            tail(3)

            w = W_STATE[3]
            inv, rr = tmp[:, 5, 0:TILES], tmp[:, 6, 0:TILES]

            def mix(k, slot):
                pooled(3, k, slot)
                x = col(X, k, D)
                row = col(PG, k, w)
                chained(v.scalar_tensor_tensor(out=per_tile(inv, k), in0=row[:, D:D + 1], scalar=0.01, in1=row[:, D + 1:D + 2],
                                               op0=ALU.add, op1=ALU.add), wait_paced)
                chained(v.reciprocal(per_tile(inv, k), per_tile(inv, k)))
                v.tensor_tensor(per_tile(rr, k), row[:, D + 1:D + 2], per_tile(inv, k), ALU.mult).then_inc(node_step, 1)
                at["n"] += 1
                chained(v.scalar_tensor_tensor(out=x, in0=row[:, 0:D], scalar=per_tile(inv, k), in1=x,
                                               op0=ALU.mult, op1=ALU.add))
                chained(v.scalar_tensor_tensor(out=x, in0=col(H, k, D), scalar=per_tile(rr, k), in1=x,
                                               op0=ALU.mult, op1=ALU.add))
                moments(X, D, k)
            chained_tiles(5, mix)
            invert()

            def own_half(k, slot):
                product(M_S_H, k)
                wait(dve, h_norm, 4 * TILES + k + 1)
                v.tensor_tensor(col(X, k, D), mm[slot % 2][:, 0:D], col(X, k, D), ALU.add).then_inc(mm_used, 1)
            tiles(dve, own_half)
            scan_pass(4)
            tail(4)

            def sage(k, slot):
                product(M_S_P, k)
                x = col(X, k, D)
                v.scalar_tensor_tensor(out=x, in0=mm[slot % 2][:, 0:D], scalar=per_tile(icnt, k), in1=x,
                                       op0=ALU.mult, op1=ALU.add).then_inc(mm_used, 1)
                wait(dve, mm_used, consumer(M_S_P)[1] + k + 1)
                moments(X, D, k)
            tiles(dve, sage)
            invert()

            mlp_pass()
            tail(5)

            def last_sum(k, slot):
                pooled(5, k, slot)
                chained(v.tensor_tensor(col(H, k, D), col(PG, k, D), col(H, k, D), ALU.add))
                moments(H, D, k)
            chained_tiles(1, last_sum)
            invert()

            def final(k, slot):
                h, x = col(H, k, D), col(X, k, D)
                wait(dve, h_norm, 6 * TILES + k + 1)
                chained(v.tensor_tensor(h, h, lnw[:, 4, :], ALU.mult))
                if isinstance(k, int) and k == 0:
                    dve.wait_ge(beta_added, TILES)
                v.tensor_tensor(x, x, h, ALU.add).then_inc(out_dve, 1)
            chained_tiles(1, final)


def kernel(x, src, dst, edge_attr_64, **w):
    import numpy as np
    import concourse.bacc as bacc
    from concourse.bass_utils import run_bass_kernel_spmd

    def pad(a, n, value=0):
        a = np.asarray(a)
        return np.concatenate([a, np.full((n - a.shape[0],) + a.shape[1:], value, a.dtype)])

    def weights(*parts):
        a = np.concatenate([np.asarray(p) for p in parts], 0)
        return a.reshape(-1, P, a.shape[1]).transpose(1, 0, 2)

    w = {k: np.asarray(v) for k, v in w.items()}
    zero_row = np.zeros(D, np.float32)
    arrays = {
        "x": pad(x, ROWS),
        "src": pad(src, EDGES).reshape(P, GROUPS, G).transpose(1, 0, 2),
        "dst": np.lib.stride_tricks.sliding_window_view(
            pad(np.concatenate([np.full(1, -1, np.int32), np.asarray(dst)]), EDGES + 1, ROWS), STEPS + 1)[::STEPS],
        "attr": pad(edge_attr_64, EDGES).reshape(P, GROUPS, G, D_EDGE).transpose(1, 3, 2, 0).reshape(GROUPS, D_EDGE, G * P),
        "w_proj": weights(w["L0_gnn_Wp1"].T), "w_l0a": weights(w["L0_gnn_Wm1"].T),
        "w_l0b": weights(w["L0_gnn_Wm2"].T), "w_l0c": weights(w["L0_gnn_Wm3"].T),
        "w_sage": weights(w["L2_gnn_W1"].T, w["L2_gnn_W2"].T), "w_q": weights(w["L1_gnn_W_dis"].T),
        "w_edge": weights(np.concatenate([w["L3_gnn_W1"][:D], w["L3_gnn_Wg"][:D]], 1)),
        "w_attr": np.concatenate([w["L3_gnn_W1"][D:], w["L3_gnn_Wg"][D:]], 1).reshape(D_EDGE, 2, D),
        "w_2": weights(w["L3_gnn_W2"]),
        "bias": np.concatenate([w[n] for n in ("L0_gnn_bp1", "L0_gnn_bm1", "L0_gnn_bm2", "L0_gnn_bm3", "L2_gnn_b1",
                                               "L2_gnn_b2", "L3_gnn_b1", "L3_gnn_bg", "L3_gnn_b2")]).reshape(1, 9, D),
        "ln": np.stack([w[n] for n in ("L0_gnn_ln2_g", "L0_gnn_ln2_b", "L0_gnn_ln3_g", "L0_gnn_ln3_b",
                                       "L3_gnn_gamma", "L3_gnn_beta")]),
    }
    arrays = {n: np.ascontiguousarray(a) for n, a in arrays.items()}
    nc = bacc.Bacc("TRN2", target_bir_lowering=False, num_devices=1)
    dram = {n: nc.dram_tensor(f"in_{n}", a.shape, mybir.dt.from_np(a.dtype), kind="ExternalInput").ap()
            for n, a in arrays.items()}
    scratch = {"states": (EDGES + 1, D), "states_wide": (EDGES + 1, D + 2), "q_edge": (EDGES + ROWS, D_Q),
               "q_node": (ROWS, D_Q)}
    scratch.update({f"table{i}": (ROWS, W_TAB[i]) for i in range(6)})
    for n, shape in scratch.items():
        dram[n] = nc.dram_tensor(n, shape, mybir.dt.float32, kind="Internal").ap()
    out = nc.dram_tensor("out", (N_NODES, D), mybir.dt.float32, kind="ExternalOutput").ap()
    build(nc, dram, out)
    r = run_bass_kernel_spmd(nc, [{f"in_{n}": a for n, a in arrays.items()}], core_ids=[0])
    return r.results[0]["out"]
```

```python
import concourse.bass as bass
from concourse import mybir
from contextlib import ExitStack

N_NODES, N_EDGES, D, D_EDGE, D_Q = 3125, 53125, 256, 64, 16
P = 128
TILES = (N_NODES + P - 1) // P
ROWS = TILES * P
STEPS = 416
EDGES = P * STEPS
G = 4
GROUPS = STEPS // G
PAIRS = STEPS // 2
FIRST_PART = 12
MEASURED = FIRST_PART + 4
TAB_DMAS = -(-TILES // 4)
OF_SLOT = [7, 6, 6, 6]
RING = 4
Q_FIRST = 2 * RING * G
IDX_RING = 8
BIG = 3.0e38
EPS = 1e-5
W_TAB = [D, D, D, D + D_Q, D, 2 * D]
W_STATE = [D, D, D, D + 2, D, D]
MAX, WSUM, SUM, MLP = "max", "weighted sum", "sum", "gated mlp"
KIND = [MAX, MAX, MAX, WSUM, SUM, MLP]
(M_PROJ, M_A_H, M_A_P, M_B_H, M_B_P, M_C_H, M_C_P, M_Q, M_S_H, M_S_P, M_EDGE) = range(11)
POOLED = (M_A_P, M_B_P, M_C_P, M_S_P)
BY_DVE = POOLED + (M_S_H,)
WGT_AT = {M_PROJ: 0, M_A_H: 2, M_A_P: 4, M_B_H: 6, M_B_P: 8, M_C_H: 10, M_C_P: 12, M_S_H: 14, M_S_P: 16}
BIASES = {M_PROJ: [0], M_A_H: [1], M_B_H: [2], M_C_H: [3], M_S_H: [4, 5], M_EDGE: [6, 7]}
B_CORE = 8
STAGE_W = {M_Q: D_Q, M_EDGE: 2 * D}


def build(nc, dram, out):
    f32, i32, bf16, f32r = mybir.dt.float32, mybir.dt.int32, mybir.dt.bfloat16, mybir.dt.float32r
    ALU, ACT, AX = mybir.AluOpType, mybir.ActivationFunctionType, mybir.AxisListType
    ds = bass.ds

    ctx = ExitStack()
    with ctx:
        def sb(name, shape, dt=f32):
            return ctx.enter_context(nc.sbuf_tensor(name, shape, dt))

        def sem(name):
            return ctx.enter_context(nc.semaphore(name))

        X = sb("X", [P, TILES * D])
        H = sb("H", [P, TILES * D])
        PG_W = STEPS * D_Q
        PG = sb("PG", [P, PG_W])
        RING_W = RING * G * 2 * D
        arena = sb("arena", [P, RING_W + 4272])
        state = sb("state", [P, RING * G, D + 2])
        with nc.sbuf_tensor("wgt_early", [P, 14, D], f32) as wgt_early:
            pass
        wedge_parts = sb("wedge_parts", [P, 4, 2 * D], f32r)
        w2_parts = sb("w2_parts", [P, 4, D], f32r)
        w2 = sb("w2", [P, 2, D])
        wgt = sb("wgt", [P, 4, D])
        wq = sb("wq", [P, 2, D_Q])
        wedge = sb("wedge", [P, 2, 2 * D])
        wattr_hi = sb("wattr_hi", [P, 2 * D], f32r)
        wattr_lo = sb("wattr_lo", [P, 2 * D], f32r)
        attr_split = sb("attr_split", [P, 2, G * P], f32r)
        bias = sb("bias", [P, 9 * D], f32r)
        bias_rows = sb("bias_rows", [P, P], f32r)
        lnw = sb("lnw", [P, 6, D])
        ident = sb("ident", [P, P])
        ones_sq = sb("ones_sq", [P, P])
        iota_lo = sb("iota_lo", [P, P], bf16)
        iota_hi = sb("iota_hi", [P, TILES], bf16)
        zeros = sb("zeros", [P, D + 2])
        aT = sb("aT", [P, 2, 2, P])
        idx = sb("idx", [P, IDX_RING * G], i32)
        dst_prev = sb("dst_prev", [P, STEPS + 1], i32)
        dsti = dst_prev[:, 1:]
        keep_sum = sb("keep_sum", [P, STEPS])
        keep_max = sb("keep_max", [P, STEPS])
        Q = sb("Q", [P, TILES * D_Q])
        qhead = sb("qhead", [P, D_Q])
        stat = sb("stat", [P, TILES * 6])
        mv = sb("mv", [P, 2, TILES])
        sd = sb("sd", [P, TILES])
        rstd = sb("rstd", [P, TILES])
        nmr = sb("nmr", [P, TILES])
        cnt = sb("cnt", [P, TILES])
        tmp = sb("tmp", [P, 8, 32])
        some = sb("some", [P, TILES])
        end_i = sb("end_i", [P, TILES], i32)
        start_i = sb("start_i", [P, TILES], i32)
        head_i = sb("head_i", [P, 1], i32)
        icnt = sb("icnt", [P, TILES])
        pcol = sb("pcol", [P, 4])
        eps_t = sb("eps_t", [P, 1])
        chain_sum = sb("chain_sum", [P, P])
        chain_max = sb("chain_max", [P, P])
        cont_max = sb("cont_max", [P, 1])
        cont_sum = sb("cont_sum", [P, 1])
        carryT = sb("carryT", [P, 3, P + 1])
        headrow = sb("headrow", [P, D + 2])
        mend = sb("mend", [P, D + 2])
        rn = sb("rn", [P, TILES])

        def slots(at, n, w):
            return arena[:, at:at + n * w].rearrange("p (s w) -> p s w", w=w)

        ring_mlp = slots(0, RING * G, 2 * D)
        ring_wide = slots(0, RING * G, D + D_Q)
        ring_one = slots(0, RING * G, D)
        RINGS = {MAX: ring_one, SUM: ring_one, WSUM: ring_wide, MLP: ring_mlp}
        Y = arena[:, RING * G * D:RING * G * D + TILES * D]
        after = RING * G * D + TILES * D
        tri = arena[:, after:after + P]
        dst_lo = arena[:, after + P:after + P + STEPS // 2].bitcast(bf16)
        dst_hi = arena[:, after + P + STEPS // 2:after + P + STEPS].bitcast(bf16)
        HOT_W = P + 32
        hot = arena[:, after + P + STEPS:after + P + STEPS + RING * G * HOT_W // 2].bitcast(bf16) \
            .rearrange("p (s w) -> p s w", w=HOT_W)
        weighted = slots(RING_W, RING * G, D + 2)
        qprod = slots(RING_W + 4128, 2 * G, D_Q)[:, 0:G, :]
        edot = arena[:, RING_W + 4256:RING_W + 4256 + G]
        msg = slots(RING_W + 1024, 2, 2 * D)
        attr_raw = slots(RING_W + 2048, 2, G * P)
        raw_bias = state[:, 0:9, 0:D]
        raw_wattr = state[:, 9:11, 0:D]

        tp = [ctx.enter_context(nc.psum_tensor(f"tp{i}", [P, 512], f32)) for i in range(2)]
        mm_pair = ctx.enter_context(nc.psum_tensor("mm_pair", [P, 1024], f32))
        mm = [mm_pair[:, 0:512], mm_pair[:, 512:1024]]
        core = [ctx.enter_context(nc.psum_tensor(f"core{i}", [P, 512], f32)) for i in range(2)]
        tailT = ctx.enter_context(nc.psum_tensor("tailT", [P, 512], f32))
        tailU = ctx.enter_context(nc.psum_tensor("tailU", [P, 512], f32))

        x_in = [sem(f"x_in{i}") for i in range(5)]
        bias_in, small_in, dst_in, w_in = sem("bias_in"), sem("small_in"), sem("dst_in"), sem("w_in")
        consts = sem("consts")
        zero_out = sem("zero_out")
        masks_done = sem("masks_done")
        prep_step = sem("prep_step")
        idx_in = [sem(f"idx_in{i}") for i in range(IDX_RING)]
        rows_in = [sem(f"rows_in{i}") for i in range(RING)]
        state_done = sem("state_done")
        dumped = [sem(f"dumped{i}") for i in range(RING)]
        hot_done, hot_used = sem("hot_done"), sem("hot_used")
        count_done, rank_done = sem("count_done"), sem("rank_done")
        count_here = sem("count_here")
        positions = sem("positions")
        chain_row, chain_rhs = sem("chain_row"), sem("chain_rhs")
        tail_T, tail_scan, tail_U = sem("tail_T"), sem("tail_scan"), sem("tail_U")
        head_in, head_out, mended = sem("head_in"), sem("head_out"), sem("mended")
        pooled_in = [sem(f"pooled_in{i}") for i in range(4)]
        qslot_out, qhead_in, qedge_in = sem("qslot_out"), sem("qhead_in"), [sem(f"qedge_in{i}") for i in range(2)]
        qedge_scan = sem("qedge_scan")
        tp_ready, at_ready, mm_ready, mm_used = (sem(n) for n in ("tp_ready", "at_ready", "mm_ready", "mm_used"))
        out_act, out_dve = sem("out_act"), sem("out_dve")
        stats_done = sem("stats_done")
        node_step = sem("node_step")
        var_ready, sd_ready, norm_ready = sem("var_ready"), sem("sd_ready"), sem("norm_ready")
        h_norm = sem("h_norm")
        tab_out = [sem(f"tab_out{i}") for i in range(5)]
        tab5_out = [sem(f"tab5_out{i}") for i in range(4)]
        bias_hi, at_low, wedge_set = sem("bias_hi"), sem("at_low"), sem("wedge_set")
        hid_low = sem("hid_low")
        bias_set, wattr_set, w2_in = sem("bias_set"), sem("wattr_set"), sem("w2_in")
        h_sum, h_scaled, x_sum = sem("h_sum"), sem("h_scaled"), sem("x_sum")
        mix_total, mix_inv, mix_share, mix_pooled = (sem(f"mix_{n}") for n in ("total", "inv", "share", "pooled"))
        relu_done = sem("relu_done")
        beta_added = sem("beta_added")
        attr_hi, attr_done = sem("attr_hi"), sem("attr_done")
        dot_step, dot_done, wrow_done = sem("dot_step"), sem("dot_done"), sem("wrow_done")
        z_ready, z_done, sig_done = sem("z_ready"), sem("z_done"), sem("sig_done")
        hT_ready, hT_done, core_ready, msg_done = (sem(n) for n in ("hT_ready", "hT_done", "core_ready", "msg_done"))
        attr_in = [sem(f"attr_in{i}") for i in range(2)]
        pace = sem("pace")
        y_out = sem("y_out")

        block = ctx.enter_context(nc.Block())

        wedge_hi, wedge_lo = wedge_parts[:, 0:2, :], wedge_parts[:, 2:4, :]
        w2_hi, w2_lo = w2_parts[:, 0:2, :], w2_parts[:, 2:4, :]
        hid_hi, hid_lo = wedge_parts[:, 0:2, :], wedge_parts[:, 2:4, :]
        hT_hi, hT_lo = (attr_split[:, i, :].rearrange("p (s w) -> p s w", w=2 * P) for i in range(2))

        def weights(at, n=1):
            return wgt_early[:, at:at + n, :] if at < 14 else wgt[:, at - 14:at - 14 + n, :]

        def col(t, k, w, n=None):
            n = w if n is None else n
            return t[:, k * w:k * w + n] if isinstance(k, int) else t[:, ds(k * w, n)]

        def tile_of(t, k):
            return t[:, k:k + 1] if isinstance(k, int) else t[:, ds(k, 1)]

        def wait(eng, s, v):
            if not isinstance(v, int) or v > 0:
                eng.wait_ge(s, v)

        def wait_paced(eng, s, v):
            wait(eng, s, v)
            if not isinstance(v, int):
                eng.sem_inc(pace)

        def tiles(eng, body, between=None, at=None, first=0, end=TILES):
            for k in range(first, first + 4):
                body(k, k % 4)
            cuts = [first // 4 + 1, end // 4]
            if between:
                cuts.insert(1, at // 4)
            for n, (a, b) in enumerate(zip(cuts, cuts[1:])):
                if n:
                    between()
                with eng.Fori(a, b) as r:
                    for i in range(4):
                        body(r * 4 + i, i)
            if end % 4:
                body(end - 1, (end - 1) % 4)

        def groups(eng, body, unroll, after_first=None):
            for g in range(unroll):
                body(g, g)
            if after_first:
                after_first()
            with eng.Fori(1, GROUPS // unroll) as r:
                for i in range(unroll):
                    body(r * unroll + i, i)

        def consumer(m):
            return (mm_used if m in BY_DVE else out_act), TILES * sum((i in BY_DVE) == (m in BY_DVE) for i in range(m))

        Q_BASE, EDGE_BASE = consumer(M_Q)[1], consumer(M_EDGE)[1]

        def earlier(g, slot, h, lag):
            d = (h - lag) // 2
            return g * 2 + (h - lag), g + d, (slot + d) % RING, (h - lag) % 2

        def used_rows(ps, g):
            return (msg_done, g * (G // 2)) if KIND[ps] == MLP else (state_done, ps * STEPS + g * G)

        def state_rows(ps):
            t = dram["states_wide"] if W_STATE[ps] > D else dram["states"]
            return t

        @block.sync
        def _(sp):
            for c in range(5):
                sp.dma_start(X[:, :].rearrange("p (k w) -> p k w", w=D)[:, 5 * c:5 * c + 5, :],
                             dram["x"].rearrange("(k p) w -> p k w", p=P)[:, 5 * c:5 * c + 5, :]).then_inc(x_in[c], 16)
            sp.dma_start(dst_prev[:, :], dram["dst"]).then_inc(dst_in, 16)
            for row in (0, D_EDGE):
                sp.dma_start(raw_wattr[row:row + D_EDGE, :, :], dram["w_attr"]).then_inc(small_in, 16)
            sp.dma_start(weights(0, 2), dram["w_proj"]).then_inc(small_in, 16)
            for at, name in ((2, "w_l0a"), (6, "w_l0b"), (10, "w_l0c"), (14, "w_sage")):
                sp.dma_start(weights(at, 4), dram[name]).then_inc(w_in, 16)
            for t, name in ((wq[:, :, :], "w_q"), (wedge[:, :, :], "w_edge")):
                sp.dma_start(t, dram[name]).then_inc(w_in, 16)
            for i in range(6):
                sp.dma_start(lnw[:, i, :], dram["ln"][i:i + 1, :].to_broadcast([P, D])).then_inc(w_in, 16)
            wait(sp, consts, 1)
            sp.dma_start(dram["states"][EDGES:EDGES + 1, :], zeros[0:1, 0:D]).then_inc(zero_out, 16)
            sp.dma_start(dram["states_wide"][EDGES:EDGES + 1, :], zeros[0:1, :]).then_inc(zero_out, 16)
            for i in range(2 * D_Q):
                half = STEPS // 2
                sp.dma_start(dram["q_edge"][0:EDGES, :].rearrange("(p t) w -> p (t w)", t=STEPS)[:, i * half:(i + 1) * half],
                             zeros[:, 0:half]).then_inc(zero_out, 16)

            def table(ps, src, s, first):
                for k in range(0, TILES, 4):
                    n = min(4, TILES - k)
                    wait(sp, s, first + k + n)
                    sp.dma_start(dram[f"table{ps}"][k * P:(k + n) * P, 0:D].rearrange("(k p) w -> p k w", p=P),
                                 src[:, k * D:(k + n) * D].rearrange("p (k w) -> p k w", w=D)).then_inc(tab_out[ps], 16)

            idx_per = GROUPS // IDX_RING

            def load_idx(g, slot):
                piece = dram["src"][g] if isinstance(g, int) else dram["src"][ds(g, 1)].rearrange("a p k -> (a p) k")
                sp.dma_start(idx[:, slot * G:slot * G + G], piece).then_inc(idx_in[slot], 16)

            def first_indices():
                for g in range(IDX_RING):
                    load_idx(g, g)

            def spool(ps):
                w = W_STATE[ps]
                rows = state_rows(ps)[0:EDGES, :].rearrange("(p t) w -> p (t w)", t=STEPS)

                def dump(g, slot):
                    wait(sp, state_done, ps * STEPS + g * G + G)
                    piece = rows[:, g * G * w:(g + 1) * G * w] if isinstance(g, int) else rows[:, ds(g * (G * w), G * w)]
                    sp.dma_start(piece.rearrange("p (t w) -> p t w", w=w),
                                 state[:, slot * G:slot * G + G, 0:w]).then_inc(dumped[slot], 16)

                def load_attr(g, slot):
                    piece = dram["attr"][g] if isinstance(g, int) else dram["attr"][ds(g, 1)].rearrange("a p k -> (a p) k")
                    for row in (0, D_EDGE):
                        sp.dma_start(attr_raw[row:row + D_EDGE, slot, :], piece).then_inc(attr_in[slot], 16)

                if KIND[ps] == MLP:
                    for g in range(2):
                        load_attr(g, g)
                lag = 2 if KIND[ps] == MLP else 0

                def body(g, slot):
                    if lag and not (isinstance(g, int) and g + 2 > GROUPS):
                        wait(sp, attr_done, g + 1)
                        load_attr(g + 2, slot % 2)
                    if not isinstance(g, int) or g >= lag:
                        dump(g - lag, (slot - lag) % RING)
                        if not isinstance(g, int) or g - lag + IDX_RING < GROUPS:
                            wait(sp, *used_rows(ps, g - lag + 1))
                            load_idx(g - lag + IDX_RING, (slot - lag) % IDX_RING)
                for g in range(IDX_RING):
                    body(g, g)
                with sp.Fori(1, idx_per - 1) as r:
                    for i in range(IDX_RING):
                        body(r * IDX_RING + i, i)
                for g in range(GROUPS - IDX_RING, GROUPS):
                    body(g, g % IDX_RING)
                for g in range(GROUPS - lag, GROUPS):
                    dump(g, g % RING)

            first_indices()
            table(0, PG, out_act, 0)
            spool(0)
            first_indices()
            table(1, H, relu_done, 0)
            spool(1)
            first_indices()
            table(2, H, out_dve, 0)
            spool(2)
            first_indices()
            table(3, H, h_norm, 3 * TILES)
            wait(sp, out_act, Q_BASE + TILES)
            q_tiles = Q[:, :].rearrange("p (k w) -> p k w", w=D_Q)
            sp.dma_start(dram["q_node"].rearrange("(k p) w -> p k w", p=P), q_tiles).then_inc(tab_out[3], 16)
            sp.dma_start(dram["table3"].rearrange("(k p) w -> p k w", p=P)[:, :, D:D + D_Q], q_tiles).then_inc(tab_out[3], 16)
            wait(sp, qslot_out, 16 * TILES)
            piece = (STEPS - Q_FIRST) // 4
            cuts = [0] + [Q_FIRST + i * piece for i in range(5)]
            for part in range(5):
                cols = slice(cuts[part] * D_Q, cuts[part + 1] * D_Q)
                sp.dma_start(PG[:, cols], dram["q_edge"][0:EDGES, :].rearrange("(p t) w -> p (t w)", t=STEPS)[:, cols]
                             ).then_inc(qedge_in[min(part, 1)], 16)
            spool(3)
            sp.dma_start(w2[:, :, :], dram["w_2"]).then_inc(w2_in, 16)
            first_indices()
            table(4, H, h_norm, 4 * TILES)
            spool(4)

            first_indices()

            def edge_table(k, slot):
                wait(sp, out_act, EDGE_BASE + k + 1)
                rows = dram["table5"][k * P:(k + 1) * P, :] if isinstance(k, int) else dram["table5"][ds(k * P, P), :]
                sp.dma_start(rows, ring_mlp[:, slot, :]).then_inc(tab5_out[slot], 16)
            tiles(sp, edge_table)
            spool(5)

            for k in range(0, TILES - 1, 4):
                wait(sp, out_dve, TILES + k + 4)
                sp.dma_start(out[k * P:(k + 4) * P, :].rearrange("(k p) w -> p k w", p=P),
                             X[:, k * D:(k + 4) * D].rearrange("p (k w) -> p k w", w=D)).then_inc(y_out, 16)
            last_rows = N_NODES - (TILES - 1) * P
            wait(sp, out_dve, 2 * TILES)
            sp.dma_start(out[(TILES - 1) * P:N_NODES, :], X[0:last_rows, (TILES - 1) * D:]).then_inc(y_out, 16)
            sp.wait_ge(y_out, 16 * TAB_DMAS)

        @block.gpsimd
        def _(pool):
            pool.memset(zeros[:, :], 0.0).then_inc(consts, 1)
            pool.memset(ones_sq[:, :], 1.0).then_inc(consts, 1)
            pool.memset(ident[:, :], 0.0).then_inc(consts, 1)
            pool.memset(tri, 1.0).then_inc(consts, 1)
            pool.memset(eps_t[:, :], EPS).then_inc(consts, 1)
            pool.memset(carryT[:, :, :], 0.0).then_inc(consts, 1)
            pool.iota(iota_lo[:, :], [[1, P]], base=0, channel_multiplier=0,
                      allow_small_or_imprecise_dtypes=True).then_inc(consts, 1)
            pool.iota(iota_hi[:, :], [[1, TILES]], base=0, channel_multiplier=0,
                      allow_small_or_imprecise_dtypes=True).then_inc(consts, 1)
            pool.iota(rn[:, :], [[P, TILES]], base=0, channel_multiplier=1,
                      allow_small_or_imprecise_dtypes=True).then_inc(consts, 1)
            pool.iota(pcol[:, 0:1], [[1, 1]], base=0, channel_multiplier=STEPS,
                      allow_small_or_imprecise_dtypes=True).then_inc(consts, 1)
            pool.memset(bias[:, :].bitcast(f32), 0.0).then_inc(consts, 1)
            pool.memset(bias_rows[:, :].bitcast(f32), 0.0).then_inc(consts, 1)
            pool.wait_ge(consts, 12)
            pool.affine_select(out=ident[:, :], in_=ident[:, :], compare_op=ALU.not_equal, fill=1.0,
                               base=0, pattern=[[-1, P]], channel_multiplier=1).then_inc(consts, 1)
            pool.affine_select(out=tri, in_=tri, compare_op=ALU.is_ge, fill=0.0,
                               base=0, pattern=[[1, P]], channel_multiplier=-1).then_inc(consts, 1)

            def run_pass(ps):
                w = W_TAB[ps]
                count = TAB_DMAS + (2 if ps == 3 else 0)
                if ps == 5:
                    for slot, s in enumerate(tab5_out):
                        pool.wait_ge(s, 16 * OF_SLOT[slot])
                else:
                    pool.wait_ge(tab_out[ps], 16 * count)
                per = GROUPS // IDX_RING

                def attr_low(g, slot):
                    wait_paced(pool, attr_hi, g + 1)
                    low = attr_split[0:D_EDGE, slot % 2, :]
                    pool.tensor_tensor(low, attr_raw[0:D_EDGE, slot % 2, :], low.bitcast(f32),
                                       ALU.subtract).then_inc(attr_done, 1)

                def body(g, slot):
                    base = (ps * per + 1) * 16
                    wait_paced(pool, idx_in[slot], base if isinstance(g, int) else (g // IDX_RING) * 16 + base)
                    if not (isinstance(g, int) and g < RING):
                        wait_paced(pool, *used_rows(ps, g - (RING - 1)))
                    rs = slot % RING
                    for i in range(G):
                        pool.indirect_dma_start(RINGS[KIND[ps]][:, rs * G + i, 0:w], None, dram[f"table{ps}"],
                                                bass.IndirectOffsetOnAxis(idx[:, slot * G + i:slot * G + i + 1], 0)
                                                ).then_inc(rows_in[rs], 16)
                    if ps == 5:
                        attr_low(g, slot)
                groups(pool, body, IDX_RING)

            def finish_pass(ps):
                w = W_STATE[ps]
                t = state_rows(ps)
                for s in dumped:
                    s_per = GROUPS // RING
                    pool.wait_ge(s, 16 * s_per * (ps + 1))
                if ps == 0:
                    pool.wait_ge(positions, 2)
                head = bass.IndirectOffsetOnAxis(head_i[:, 0:1], 0)
                if KIND[ps] == MAX:
                    pool.indirect_dma_start(headrow[:, 0:w], None, t, head).then_inc(head_in, 16)
                    pool.wait_ge(mended, ps + 1)
                    pool.indirect_dma_start(t, head, mend[:, 0:w], None).then_inc(head_out, 16)
                else:
                    pool.wait_ge(mended, ps + 1)
                    pool.indirect_dma_start(t, head, mend[:, 0:w], None, compute_op=ALU.add).then_inc(head_out, 16)
                pool.wait_ge(head_out, 16 * (ps + 1))
                if ps == 0:
                    pool.wait_ge(zero_out, 16 * (2 + 2 * D_Q))
                for k in range(TILES):
                    i, r = k % 4, k // 4
                    before = 16 * (ps * OF_SLOT[i] + r)
                    if before:
                        pool.wait_ge(pooled_in[i], before)
                    pool.indirect_dma_start(PG[:, k * w:k * w + w], None, t,
                                            bass.IndirectOffsetOnAxis(end_i[:, k:k + 1], 0)).then_inc(pooled_in[i], 16)

            for ps in range(6):
                if ps == 3:
                    for k in range(TILES):
                        pool.wait_ge(out_act, Q_BASE + k + 1)
                        pool.indirect_dma_start(dram["q_edge"], bass.IndirectOffsetOnAxis(start_i[:, k:k + 1], 0),
                                                Q[:, k * D_Q:(k + 1) * D_Q], None).then_inc(qslot_out, 16)
                    pool.wait_ge(tab_out[3], 16 * (TAB_DMAS + 2))
                    pool.indirect_dma_start(qhead[:, :], None, dram["q_node"],
                                            bass.IndirectOffsetOnAxis(dst_prev[:, 1:2], 0)).then_inc(qhead_in, 16)
                if ps == 5:
                    def add_beta(k, slot):
                        wait_paced(pool, h_norm, 5 * TILES + k + 1)
                        x = col(X, k, D)
                        pool.tensor_tensor(x, x, lnw[:, 5, :], ALU.add).then_inc(beta_added, 1)
                    tiles(pool, add_beta)
                run_pass(ps)
                finish_pass(ps)

        @block.tensor
        def _(pe):
            def stage(m, ready):
                w, base = STAGE_W.get(m, D), m * TILES
                used, used_base = consumer(m)
                src = PG if m in POOLED else H

                def transposes(k, slot):
                    ready(k, slot)
                    wait(pe, at_ready, base + max(k - 1, 0))
                    if m == M_EDGE:
                        wait(pe, at_low, k - 1)
                    for c in range(2):
                        last = nc.tensor.transpose(tp[slot % 2][:, c * P:(c + 1) * P],
                                                   src[:, k * D + c * P:k * D + c * P + P], ident[:, :])
                    last.then_inc(tp_ready, 1)

                def multiply(k, slot):
                    wait(pe, at_ready, base + k + 1)
                    if k == 0 and m > 0:
                        before, before_base = consumer(m - 1)
                        wait(pe, before, before_base + TILES)
                    wait(pe, used, used_base + max(k - 1, 0))
                    o = mm[slot % 2][:, 0:w]
                    rows = BIASES.get(m, [])
                    if m == M_EDGE:
                        wait(pe, at_low, k + 1)
                        for n, (left, right) in enumerate(((hT_hi, wedge_hi), (hT_hi, wedge_lo), (hT_lo, wedge_hi))):
                            for c in range(2):
                                nc.tensor.matmul(o, left[:, slot % 2, c * P:(c + 1) * P], right[:, c, :],
                                                 start=(n == c == 0), stop=False)
                        last = nc.tensor.matmul(o, bias_rows[:, :], bias[:, rows[0] * D:(rows[-1] + 1) * D], start=False, stop=True)
                    else:
                        for c in range(2):
                            rhs = wq[:, c, :] if m == M_Q else weights(WGT_AT[m] + c)[:, 0, :]
                            last = nc.tensor.matmul(o, aT[:, slot % 2, c, :], rhs, start=(c == 0), stop=(c == 1 and not rows))
                        for n, b in enumerate(rows):
                            last = nc.tensor.matmul(o, bias_rows[:, :], bias[:, b * D:(b + 1) * D], start=False,
                                                    stop=(n == len(rows) - 1))
                    last.then_inc(mm_ready, 1)

                for k in range(TILES):
                    transposes(k, k % 4)
                    if k:
                        multiply(k - 1, (k - 1) % 4)
                multiply(TILES - 1, 0)

            def nothing(k, slot):
                pass

            def pooled(ps):
                def ready(k, slot):
                    n = OF_SLOT[slot]
                    wait(pe, pooled_in[slot], (k // 4) * 16 + 16 * (ps * n + 1))
                return ready

            def counts():
                o = tailU[:, 0:TILES]
                nc.tensor.matmul(o, ones_sq[:, :], zeros[:, 0:TILES], start=True, stop=False)

                def body(g, slot):
                    wait(pe, hot_done, g * G + G)
                    for i in range(G):
                        row = hot[:, slot * G + i, :]
                        last = nc.tensor.matmul(o, row[:, 0:P], row[:, P:P + TILES], start=False, stop=False)
                    last.then_inc(hot_used, 1)
                groups(pe, body, RING)
                nc.tensor.matmul(o, ones_sq[:, :], zeros[:, 0:TILES], start=False, stop=True).then_inc(count_done, 1)
                pe.wait_ge(count_here, 1)
                nc.tensor.matmul(tailU[:, 64:64 + TILES], tri, cnt[:, :], start=True, stop=True)
                nc.tensor.matmul(tailU[:, 128:128 + TILES], ones_sq[:, :], cnt[:, :], start=True, stop=True).then_inc(rank_done, 1)
                pe.wait_ge(chain_rhs, 1)
                pe.wait_ge(positions, 1)
                nc.tensor.matmul(tailU[:, 256:384], ones_sq[:, :], chain_sum[:, :], start=True, stop=True).then_inc(chain_row, 1)

            def tail(ps):
                w = W_STATE[ps]
                pe.wait_ge(state_done, STEPS * (ps + 1))
                if ps == 0:
                    pe.wait_ge(positions, 2)
                blocks = [(0, P), (P, P)] + ([(2 * P, 2)] if w > D else [])
                for b, (at, n) in enumerate(blocks):
                    last = nc.tensor.transpose(tailT[0:n, b * P:(b + 1) * P], state[:, RING * G - 1, at:at + n], ident[:, :])
                last.then_inc(tail_T, 1)
                pe.wait_ge(tail_scan, 3 * ps + 3)
                for b, (at, n) in enumerate(blocks):
                    last = nc.tensor.transpose(tailU[:, at:at + n], carryT[0:n, b, 0:P], ident[0:n, 0:n])
                last.then_inc(tail_U, 1)

            def edge_mlp():
                pe.wait_ge(out_act, EDGE_BASE + TILES)
                pe.wait_ge(wedge_set, 4)

                def attr_part(u, g, slot, h):
                    if h == 0:
                        wait(pe, attr_done, g + 1)
                    wait(pe, z_done, u)
                    for i in range(2):
                        rows = attr_split[:, slot % 2, (2 * h + i) * P:(2 * h + i + 1) * P]
                        nc.tensor.matmul(mm[i], rows, wattr_hi[:, :], start=True, stop=False)
                        last = nc.tensor.matmul(mm[i], rows, wattr_lo[:, :], start=False, stop=True)
                    last.then_inc(z_ready, 1)

                def hidden_T(u, slot, h):
                    wait(pe, z_done, u + 1)
                    wait(pe, hT_done, u - 1)
                    wait(pe, hid_low, u - 1)
                    for i in range(2):
                        for c in range(2):
                            last = nc.tensor.transpose(tp[h][:, (2 * i + c) * P:(2 * i + c + 1) * P],
                                                       ring_mlp[:, slot * G + 2 * h + i, c * P:(c + 1) * P], ident[:, :])
                    last.then_inc(hT_ready, 1)

                def core_part(u, slot, h):
                    wait(pe, hid_low, u + 1)
                    wait(pe, msg_done, u - 1)
                    for i in range(2):
                        o = core[h][:, i * D:(i + 1) * D]
                        for n, (left, right) in enumerate(((hid_hi, w2_hi), (hid_hi, w2_lo), (hid_lo, w2_hi))):
                            for c in range(2):
                                nc.tensor.matmul(o, left[:, h, (2 * i + c) * P:(2 * i + c + 1) * P], right[:, c, :],
                                                 start=(n == c == 0), stop=False)
                        last = nc.tensor.matmul(o, bias_rows[:, :], bias[:, B_CORE * D:(B_CORE + 1) * D], start=False, stop=True)
                    last.then_inc(core_ready, 1)

                def body(g, slot):
                    for h in range(2):
                        attr_part(g * 2 + h, g, slot, h)
                        for lag, part in ((1, hidden_T), (2, core_part)):
                            u, _, s, hh = earlier(g, slot, h, lag)
                            if not isinstance(u, int) or u >= 0:
                                part(u, s, hh)
                groups(pe, body, RING)
                hidden_T(PAIRS - 1, RING - 1, 1)
                core_part(PAIRS - 2, RING - 1, 0)
                core_part(PAIRS - 1, RING - 1, 1)

            pe.wait_ge(consts, 14)
            pe.wait_ge(bias_hi, 2)
            pe.wait_ge(bias_set, 3)
            pe.wait_ge(small_in, 16 * 3)
            stage(M_PROJ, lambda k, slot: wait(pe, h_norm, k + 1))
            pe.wait_ge(w_in, 16 * 12)
            stage(M_A_H, nothing)
            counts()
            tail(0)
            stage(M_A_P, pooled(0))
            stage(M_B_H, lambda k, slot: wait(pe, relu_done, k + 1))
            tail(1)
            stage(M_B_P, pooled(1))
            stage(M_C_H, lambda k, slot: wait(pe, out_dve, k + 1))
            tail(2)
            stage(M_C_P, pooled(2))
            stage(M_Q, lambda k, slot: wait(pe, h_norm, 3 * TILES + k + 1))
            tail(3)
            stage(M_S_H, lambda k, slot: wait(pe, h_norm, 4 * TILES + k + 1))
            tail(4)
            stage(M_S_P, pooled(4))
            pe.wait_ge(wedge_set, 2)
            stage(M_EDGE, lambda k, slot: wait(pe, h_norm, 5 * TILES + k + 1))
            pe.wait_ge(wattr_set, 2)
            edge_mlp()
            tail(5)

        @block.scalar
        def _(act):
            def normalised(func, src, dst, k):
                nc.scalar.activation(col(dst, k, D), col(src, k, D), func, bias=tile_of(nmr, k),
                                     scale=tile_of(rstd, k)).then_inc(h_norm, 1)

            def stage(m, output, norm=None, between=None):
                base = m * TILES

                def copy_T(k, slot):
                    wait(act, tp_ready, base + k + 1)
                    if isinstance(k, int):
                        wait(act, mm_ready, base + max(k - 1, 0))
                    else:
                        wait(act, mm_ready, base + k - 1)
                    to = hT_hi[:, slot % 2, :] if m == M_EDGE else aT[:, slot % 2, :, :].rearrange("p c n -> p (c n)")
                    nc.scalar.activation(to, tp[slot % 2][:, 0:2 * P], ACT.Copy).then_inc(at_ready, 1)

                lag = 2 if norm else 0
                if norm:
                    act.wait_ge(norm_ready, norm[0])

                def body(k, slot):
                    if norm and not (isinstance(k, int) and k >= TILES):
                        normalised(norm[1], norm[2], H, k)
                    if not isinstance(k, int) or k >= lag:
                        copy_T(k - lag, (slot - lag) % 4)
                    if output and (not isinstance(k, int) or k > lag):
                        output(k - lag - 1, (slot - lag - 1) % 4)
                tiles(act, body, between=between, at=FIRST_PART)
                for k in range(TILES, TILES + lag):
                    body(k, k % 4)
                if output:
                    output(TILES - 1, 0)

            def root(n, first=0, end=TILES):
                act.wait_ge(var_ready, n)
                nc.scalar.activation(sd[:, first:end], mv[:, 1, first:end], ACT.Sqrt,
                                     bias=eps_t[:, 0:1]).then_inc(sd_ready, 1)

            def normalise(n, func, src, dst, between=None):
                act.wait_ge(norm_ready, n)

                tiles(act, lambda k, slot: normalised(func, src, dst, k), between=between, at=FIRST_PART)

            def product_to(m, dst, func):
                def output(k, slot):
                    wait(act, mm_ready, m * TILES + k + 1)
                    nc.scalar.activation(col(dst, k, D), mm[slot % 2][:, 0:D], func).then_inc(out_act, 1)
                return output

            def relu_y(k, slot):
                wait(act, mm_used, consumer(M_A_P)[1] + k + 1)
                nc.scalar.activation(col(H, k, D), col(Y, k, D), ACT.Relu).then_inc(relu_done, 1)

            def weigh_rows():
                def body(g, slot):
                    wait(act, dot_done, g + 1)
                    if not (isinstance(g, int) and g < RING):
                        wait(act, state_done, 3 * STEPS + (g - (RING - 1)) * G)
                    for i in range(G):
                        s = slot * G + i
                        last = nc.scalar.activation(weighted[:, s, 0:D], ring_wide[:, s, 0:D], ACT.Copy,
                                                    scale=weighted[:, s, D:D + 1])
                        last.then_inc(wrow_done, 1)
                groups(act, body, RING)

            def edge_gates():
                def attr_high(g, slot):
                    wait(act, attr_in[slot % 2], (g - slot % 2) * 16 + 32)
                    wait(act, z_ready, g * 2 - 2)
                    nc.scalar.activation(attr_split[:, slot % 2, :], attr_raw[:, slot % 2, :], ACT.Copy).then_inc(attr_hi, 1)

                def gate(u, slot, h):
                    wait(act, z_done, u + 1)
                    z = ring_mlp[:, slot * G + 2 * h:slot * G + 2 * h + 2, D:2 * D]
                    nc.scalar.activation(z, z, ACT.Sigmoid).then_inc(sig_done, 1)

                def hidden(u, slot, h):
                    wait(act, hT_ready, u + 1)
                    wait(act, core_ready, u - 1)
                    nc.scalar.activation(hid_hi[:, h, :], tp[h][:, :], ACT.Relu).then_inc(hT_done, 1)

                attr_high(0, 0)

                def body(g, slot):
                    for h in range(2):
                        u, _, s, hh = earlier(g, slot, h, 1)
                        if not isinstance(u, int) or u >= 0:
                            gate(u, s, hh)
                            hidden(u, s, hh)
                        if h == 0:
                            attr_high(g + 1, slot + 1)
                groups(act, body, RING)
                gate(PAIRS - 1, RING - 1, 1)
                hidden(PAIRS - 1, RING - 1, 1)

            for row in (0, 32):
                act.dma_start(raw_bias[row:row + 1, :, :], dram["bias"]).then_inc(bias_in, 16)
            act.wait_ge(consts, 14)
            for row in (0, 32):
                nc.scalar.activation(bias_rows[row:row + 1, :], ones_sq[row:row + 1, :], ACT.Copy).then_inc(bias_set, 1)
            act.wait_ge(bias_in, 16 * 2)
            for row in (32, 0):
                nc.scalar.activation(bias[row:row + 1, :].rearrange("p (b w) -> p b w", w=D), raw_bias[row:row + 1, :, :],
                                     ACT.Copy).then_inc(bias_hi, 1)

            def second_part(n):
                def roots():
                    root(n, FIRST_PART, TILES)
                    act.wait_ge(norm_ready, n)
                return roots
            root(1, 0, FIRST_PART)
            stage(M_PROJ, product_to(M_PROJ, PG, ACT.Relu), (1, ACT.Relu, X), second_part(2))
            stage(M_A_H, product_to(M_A_H, Y, ACT.Copy))
            stage(M_A_P, relu_y)
            stage(M_B_H, product_to(M_B_H, Y, ACT.Copy))
            stage(M_B_P, None)
            root(3)
            normalise(3, ACT.Identity, H, H)
            stage(M_C_H, product_to(M_C_H, Y, ACT.Copy))
            stage(M_C_P, None)
            root(4)
            normalise(4, ACT.Identity, H, H)
            root(5, 0, FIRST_PART)

            def scaled_q(k, slot):
                wait(act, mm_ready, M_Q * TILES + k + 1)
                nc.scalar.activation(col(Q, k, D_Q), mm[slot % 2][:, 0:D_Q], ACT.Copy, scale=0.25).then_inc(out_act, 1)
            stage(M_Q, scaled_q, (5, ACT.Relu, X), second_part(6))
            weigh_rows()
            root(7, 0, FIRST_PART)
            normalise(7, ACT.Relu, X, H, second_part(8))
            stage(M_S_H, None)
            stage(M_S_P, None)
            root(9)

            def staged(k, slot):
                wait(act, mm_ready, M_EDGE * TILES + k + 1)
                if not (isinstance(k, int) and k < 4):
                    wait(act, tab5_out[slot], (k // 4) * 16)
                nc.scalar.activation(ring_mlp[:, slot, :], mm[slot % 2][:, :], ACT.Copy).then_inc(out_act, 1)
            stage(M_EDGE, staged, (9, ACT.Relu, X))
            edge_gates()
            root(10, 0, FIRST_PART)
            normalise(10, ACT.Identity, H, H, second_part(11))

        @block.vector
        def _(dve):
            v = nc.vector
            steps = [0]

            def prep(ins):
                steps[0] += 1
                ins.then_inc(prep_step, 1)
                dve.wait_ge(prep_step, steps[0])

            node_steps = [0]

            def chained(ins, last=True):
                node_steps[0] += 1
                ins.then_inc(node_step, 1)
                if last:
                    dve.wait_ge(node_step, node_steps[0])

            def moments(src, w, k):
                v.bn_stats(col(stat, k, 6), col(src, k, w, D)).then_inc(stats_done, 1)

            def pipeline(*parts, between=None, first=0, end=TILES):
                def body(k, slot, from_part=0):
                    for j, (part, done, base) in enumerate(parts):
                        if j < from_part or (isinstance(k, int) and k - j < first):
                            continue
                        if j:
                            wait(dve, parts[j - 1][1], parts[j - 1][2] + k - j + 1)
                        part(k - j, (slot - j) % 4).then_inc(done, 1)
                tiles(dve, body, between, MEASURED, first, end)
                for j in range(1, len(parts)):
                    body(end - 1 + j, (end - 1 + j) % 4, from_part=j)

            def moments_of(src, w):
                return (lambda k, slot: v.bn_stats(col(stat, k, 6), col(src, k, w, D))), stats_done, 0

            norms, measured = [0], [0]

            def invert(first=0, end=TILES):
                norms[0] += 1
                measured[0] += end - first
                dve.wait_ge(stats_done, measured[0])
                s3 = stat[:, first * 6:end * 6].rearrange("p (k c) -> p k c", c=6)
                total, var = mv[:, 0, first:end], mv[:, 1, first:end]
                root, scale, shift = sd[:, first:end], rstd[:, first:end], nmr[:, first:end]
                mean_e, dev_e, mean_o, dev_o = (s3[:, :, c] for c in (1, 2, 4, 5))
                chained(v.tensor_tensor(total, mean_e, mean_o, ALU.add), last=False)
                chained(v.tensor_tensor(var, dev_e, dev_o, ALU.add), last=False)
                chained(v.tensor_tensor(root, mean_e, mean_o, ALU.subtract))
                chained(v.tensor_tensor(root, root, root, ALU.mult))
                chained(v.tensor_scalar(root, root, 0.25, None, ALU.mult))
                chained(v.scalar_tensor_tensor(out=var, in0=var, scalar=1.0 / D, in1=root,
                                               op0=ALU.mult, op1=ALU.add))
                v.engine_nop().then_inc(var_ready, 1)
                dve.wait_ge(sd_ready, norms[0])
                chained(v.reciprocal(scale, root))
                v.scalar_tensor_tensor(out=shift, in0=total, scalar=-0.5, in1=scale,
                                       op0=ALU.mult, op1=ALU.mult).then_inc(norm_ready, 1)
                dve.wait_ge(norm_ready, norms[0])

            for k in range(TILES):
                if k % 5 == 0:
                    dve.wait_ge(x_in[k // 5], 16)
                if k == 15:
                    dve.wait_ge(bias_hi, 2)
                    low = bias[32:33, :].rearrange("p (b w) -> p b w", w=D)
                    v.tensor_tensor(low, raw_bias[32:33, :, :], low.bitcast(f32), ALU.subtract).then_inc(bias_set, 1)
                if k == FIRST_PART:
                    invert(0, FIRST_PART)
                moments(X, D, k)
            invert(FIRST_PART, TILES)
            dve.wait_ge(consts, 14)

            dve.wait_ge(small_in, 16 * 3)
            hi3, lo3 = (t[:, :].rearrange("p (b w) -> p b w", w=D) for t in (wattr_hi, wattr_lo))
            v.tensor_copy(hi3, raw_wattr).then_inc(wattr_set, 1)
            dve.wait_ge(wattr_set, 1)
            v.tensor_tensor(lo3, raw_wattr, hi3.bitcast(f32), ALU.subtract).then_inc(wattr_set, 1)

            dve.wait_ge(dst_in, 16)
            prep(v.memset(keep_sum[:, 0:1], 0.0))
            prep(v.tensor_tensor(keep_sum[:, 1:], dsti[:, 1:], dsti[:, 0:STEPS - 1], ALU.is_equal))
            v.tensor_scalar(keep_max[:, :], keep_sum[:, :], -1.0, BIG, ALU.add, ALU.mult).then_inc(masks_done, 1)
            dve.wait_ge(masks_done, 1)

            flat = state[:, :, :].rearrange("p s w -> p (s w)")
            lo_i = flat[:, 0:STEPS].bitcast(i32)
            hi_i = flat[:, 512:512 + STEPS].bitcast(i32)
            eq = flat[:, 1024:1024 + STEPS]
            prep(v.tensor_scalar(lo_i, dsti, P - 1, None, ALU.bitwise_and))
            prep(v.tensor_scalar(hi_i, dsti, 7, None, ALU.logical_shift_right))
            prep(v.tensor_copy(dst_lo, lo_i))
            prep(v.tensor_copy(dst_hi, hi_i))
            prep(v.tensor_copy(pcol[:, 1:2], dsti[:, 0:1]))
            prep(v.tensor_tensor(cont_sum[:, :], dsti[:, 0:1], dst_prev[:, 0:1], ALU.is_equal))
            prep(v.tensor_scalar(cont_max[:, :], cont_sum[:, :], -1.0, BIG, ALU.add, ALU.mult))
            prep(v.tensor_copy(eq, dsti))
            prep(v.tensor_scalar(eq, eq, pcol[:, 1:2], None, ALU.is_equal))
            prep(v.tensor_reduce(pcol[:, 3:4], eq, AX.X, ALU.add))
            prep(v.scalar_tensor_tensor(out=tmp[:, 0, 0:1], in0=pcol[:, 3:4], scalar=-1.0, in1=pcol[:, 0:1],
                                        op0=ALU.add, op1=ALU.add))
            prep(v.tensor_copy(head_i[:, :], tmp[:, 0, 0:1]))
            prep(v.scalar_tensor_tensor(out=tmp[:, 1, 0:1], in0=pcol[:, 3:4], scalar=float(STEPS), in1=cont_sum[:, :],
                                        op0=ALU.is_equal, op1=ALU.mult))
            v.tensor_scalar(chain_sum[:, :], ident[:, :], tmp[:, 1, 0:1], None, ALU.mult).then_inc(chain_rhs, 1)

            def scan_step(ps, t, slot, t_mask, src):
                w = W_STATE[ps]
                if isinstance(t, int) and t == 0:
                    v.tensor_copy(state[:, slot, 0:w], src).then_inc(state_done, 1)
                    return
                wait(dve, state_done, ps * STEPS + t)
                mask, op0, op1 = (keep_max, ALU.add, ALU.max) if KIND[ps] == MAX else (keep_sum, ALU.mult, ALU.add)
                v.scalar_tensor_tensor(out=state[:, slot, 0:w], in0=state[:, (slot - 1) % (RING * G), 0:w],
                                       scalar=tile_of(mask, t_mask), in1=src, op0=op0, op1=op1).then_inc(state_done, 1)

            def slot_free(ps, g, slot):
                wait(dve, dumped[slot], (ps * (GROUPS // RING) + g // RING) * 16)

            def rows_there(ps, g, slot):
                wait(dve, rows_in[slot], (ps * (GROUPS // RING) + g // RING + 1) * (16 * G))

            def scan_pass(ps, beside=None):
                w = W_STATE[ps]

                def body(g, slot):
                    if ps == 0:
                        wait(dve, hot_used, g - (RING - 1) if not isinstance(g, int) else max(g - (RING - 1), 0))
                        for i in range(G):
                            row = hot[:, slot * G + i, :]
                            v.tensor_scalar(row[:, 0:P], iota_lo[:, :], tile_of(dst_lo, g * G + i), None, ALU.is_equal)
                            v.tensor_scalar(row[:, P:P + TILES], iota_hi[:, :], tile_of(dst_hi, g * G + i), None,
                                            ALU.is_equal).then_inc(hot_done, 1)
                    rows_there(ps, g, slot)
                    slot_free(ps, g, slot)
                    for i in range(G):
                        scan_step(ps, g * G + i, slot * G + i, g * G + i, RINGS[KIND[ps]][:, slot * G + i, 0:w])
                if not beside:
                    groups(dve, body, RING)
                    return

                def both(g, slot):
                    body(g, slot)
                    beside(g, slot)
                tiles(dve, both)
                for g in range(TILES, TILES + 3):
                    body(g, g % RING)
                with dve.Fori(TILES // RING + 1, GROUPS // RING) as r:
                    for i in range(RING):
                        body(r * RING + i, i)

            def weighted_pass(after_first):
                ps = 3

                def dots(g, slot):
                    rows_there(ps, g, slot)
                    if not (isinstance(g, int) and g < RING):
                        wait(dve, state_done, ps * STEPS + (g - RING + 1) * G)
                    n = g * 3
                    rs = slice(slot * G, slot * G + G)
                    qd = PG[:, g * G * D_Q:(g + 1) * G * D_Q] if isinstance(g, int) else PG[:, ds(g * (G * D_Q), G * D_Q)]
                    v.tensor_tensor(qprod, ring_wide[:, rs, D:D + D_Q], qd.rearrange("p (t w) -> p t w", w=D_Q),
                                    ALU.mult).then_inc(dot_step, 1)
                    wait(dve, dot_step, n + 1)
                    v.tensor_reduce(edot, qprod, AX.X, ALU.add).then_inc(dot_step, 1)
                    wait(dve, dot_step, n + 2)
                    v.tensor_scalar(weighted[:, rs, D + 1], edot, -1.0, 0.0, ALU.mult, ALU.max).then_inc(dot_step, 1)
                    wait(dve, dot_step, n + 3)
                    v.tensor_scalar(weighted[:, rs, D], edot, 0.0, None, ALU.max).then_inc(dot_done, 1)

                def scans(g, slot):
                    slot_free(ps, g, slot)
                    for i in range(G):
                        wait(dve, wrow_done, g * G + i + 1)
                        scan_step(ps, g * G + i, slot * G + i, g * G + i, weighted[:, slot * G + i, :])

                def body(g, slot):
                    dots(g, slot)
                    if not (isinstance(g, int) and g == 0):
                        scans(g - 1, (slot - 1) % RING)
                groups(dve, body, RING, after_first)
                scans(GROUPS - 1, RING - 1)

            def mlp_pass():
                ps = 5
                dve.wait_ge(out_act, EDGE_BASE + TILES)

                def add(u, g, slot, h):
                    if h == 0:
                        rows_there(ps, g, slot)
                    wait(dve, z_ready, u + 1)
                    z = ring_mlp[:, slot * G + 2 * h:slot * G + 2 * h + 2, :]
                    v.tensor_tensor(z, mm_pair[:, :].rearrange("p (s w) -> p s w", w=2 * D), z, ALU.add).then_inc(z_done, 1)

                def low(u, g, slot, h):
                    wait(dve, hT_done, u + 1)
                    v.scalar_tensor_tensor(out=hid_lo[:, h, :], in0=tp[h][:, :], scalar=0.0, in1=hid_hi[:, h, :].bitcast(f32),
                                           op0=ALU.max, op1=ALU.subtract).then_inc(hid_low, 1)

                def message(u, g, slot, h):
                    s = slot * G + 2 * h
                    wait(dve, core_ready, u + 1)
                    wait(dve, sig_done, u + 1)
                    v.tensor_tensor(msg[:, h, :].rearrange("p (s w) -> p s w", w=D),
                                    core[h][:, :].rearrange("p (s w) -> p s w", w=D),
                                    ring_mlp[:, s:s + 2, D:2 * D], ALU.mult).then_inc(msg_done, 1)

                def scan(u, g, slot, h, i):
                    if h == 0 and i == 0:
                        slot_free(ps, g, slot)
                    if i == 0:
                        wait(dve, msg_done, u + 1)
                    scan_step(ps, u * 2 + i, slot * G + 2 * h + i, u * 2 + i, msg[:, h, i * D:(i + 1) * D])

                def turn(g, slot, h, first=0, last=4):
                    back = {lag: earlier(g, slot, h, lag) for lag in (1, 2, 3, 4)}
                    exists = {lag: (not isinstance(b[0], int) or b[0] >= 0) and first <= lag <= last
                              for lag, b in back.items()}
                    if exists[1]:
                        add(*back[1])
                    if exists[2]:
                        low(*back[2])
                    if exists[4]:
                        scan(*back[4], 0)
                    if exists[3]:
                        message(*back[3])
                    if exists[4]:
                        scan(*back[4], 1)

                def body(g, slot):
                    for h in range(2):
                        turn(g, slot, h)
                groups(dve, body, RING)
                turn(GROUPS, 0, 0)
                turn(GROUPS, 0, 1, first=2)
                turn(GROUPS + 1, 1, 0, first=3)
                turn(GROUPS + 1, 1, 1, first=4)

            def tail(ps):
                w = W_STATE[ps]
                wide = w > D
                row = chain_max if KIND[ps] == MAX else chain_sum
                op0, op1 = (ALU.add, ALU.max) if KIND[ps] == MAX else (ALU.mult, ALU.add)
                dve.wait_ge(tail_T, ps + 1)
                for b in range(3):
                    n = P if b < 2 else 2
                    if b == 2 and not wide:
                        v.engine_nop().then_inc(tail_scan, 1)
                        continue
                    v.tensor_tensor_scan(carryT[0:n, b, 1:P + 1], row[0:n, :], tailT[0:n, b * P:(b + 1) * P], 0.0,
                                         op0, op1).then_inc(tail_scan, 1)
                dve.wait_ge(tail_U, ps + 1)
                if ps:
                    dve.wait_ge(head_out, 16 * ps)
                if KIND[ps] == MAX:
                    dve.wait_ge(head_in, 16 * (ps + 1))
                    v.scalar_tensor_tensor(out=mend[:, 0:w], in0=tailU[:, 0:w], scalar=cont_max[:, 0:1],
                                           in1=headrow[:, 0:w], op0=op0, op1=op1).then_inc(mended, 1)
                else:
                    v.tensor_scalar(mend[:, 0:w], tailU[:, 0:w], cont_sum[:, 0:1], None, ALU.mult).then_inc(mended, 1)

            def pooled(ps, k, slot):
                n = OF_SLOT[slot]
                wait(dve, pooled_in[slot], (k // 4) * 16 + 16 * (ps * n + 1))

            def product(m, k):
                wait(dve, mm_ready, m * TILES + k + 1)

            dve.wait_ge(prep_step, steps[0])
            scan_pass(0)
            dve.wait_ge(count_done, 1)
            v.tensor_copy(cnt[:, :], tailU[:, 0:TILES]).then_inc(count_here, 1)
            dve.wait_ge(rank_done, 1)
            total, within = tmp[:, 2, 0:TILES], tmp[:, 3, 0:TILES]
            prep(v.tensor_copy(total, tailU[:, 128:128 + TILES]))
            prep(v.tensor_copy(within, tailU[:, 64:64 + TILES]))
            prep(v.tensor_tensor_scan(tmp[:, 4, 0:TILES], ones_sq[:, 0:TILES], total, 0.0, ALU.mult, ALU.add))
            prep(v.tensor_tensor(tmp[:, 4, 0:TILES], tmp[:, 4, 0:TILES], total, ALU.subtract))
            prep(v.tensor_tensor(within, within, tmp[:, 4, 0:TILES], ALU.add))
            prep(v.tensor_scalar(some[:, :], cnt[:, :], 1.0, None, ALU.min))
            prep(v.tensor_scalar(tmp[:, 5, 0:TILES], within, float(-1 - EDGES), None, ALU.add))
            prep(v.tensor_tensor(tmp[:, 5, 0:TILES], tmp[:, 5, 0:TILES], some[:, :], ALU.mult))
            prep(v.tensor_scalar(tmp[:, 5, 0:TILES], tmp[:, 5, 0:TILES], float(EDGES), None, ALU.add))
            prep(v.tensor_copy(end_i[:, :], tmp[:, 5, 0:TILES]))
            prep(v.tensor_tensor(within, within, cnt[:, :], ALU.subtract))
            prep(v.tensor_scalar(rn[:, :], rn[:, :], float(EDGES), None, ALU.add))
            prep(v.tensor_tensor(within, within, rn[:, :], ALU.subtract))
            prep(v.tensor_tensor(within, within, some[:, :], ALU.mult))
            prep(v.tensor_tensor(within, within, rn[:, :], ALU.add))
            prep(v.tensor_copy(start_i[:, :], within))
            prep(v.tensor_scalar(icnt[:, :], cnt[:, :], 1.0, None, ALU.max))
            prep(v.reciprocal(icnt[:, :], icnt[:, :]))
            v.engine_nop().then_inc(positions, 1)
            dve.wait_ge(chain_row, 1)
            prep(v.tensor_copy(chain_sum[:, :], tailU[:, 256:384]))
            prep(v.tensor_scalar(chain_max[:, :], chain_sum[:, :], -1.0, BIG, ALU.add, ALU.mult))
            v.engine_nop().then_inc(positions, 1)
            tail(0)

            def sum_halves(m):
                def add(k, slot):
                    product(m, k)
                    return v.tensor_tensor(col(Y, k, D), mm[slot % 2][:, 0:D], col(Y, k, D), ALU.add)
                return add, mm_used, consumer(m)[1]

            def relu_and_add(k, slot):
                return v.scalar_tensor_tensor(out=col(H, k, D), in0=col(Y, k, D), scalar=0.0, in1=col(H, k, D),
                                              op0=ALU.max, op1=ALU.add)

            def first(k, slot):
                product(M_A_P, k)
                y = col(Y, k, D)
                v.tensor_tensor(y, mm[slot % 2][:, 0:D], y, ALU.add).then_inc(mm_used, 1)
            tiles(dve, first)
            scan_pass(1)
            tail(1)

            dve.wait_ge(w_in, 16 * 12)
            pipeline(sum_halves(M_B_P), (relu_and_add, h_sum, 0), moments_of(H, D))
            invert()

            def times_weight(row, n):
                def mult(k, slot):
                    wait(dve, h_norm, n * TILES + k + 1)
                    return v.tensor_tensor(col(H, k, D), col(H, k, D), lnw[:, row, :], ALU.mult)
                return mult

            def plus_shift(k, slot):
                return v.tensor_tensor(col(H, k, D), col(H, k, D), lnw[:, 1, :], ALU.add)
            pipeline((times_weight(0, 1), h_scaled, 0), (plus_shift, out_dve, 0))

            def shift_x(k, slot):
                return v.tensor_tensor(col(X, k, D), col(X, k, D), lnw[:, 3, :], ALU.add)
            pipeline((shift_x, x_sum, 0))
            scan_pass(2)
            tail(2)

            pipeline(sum_halves(M_C_P), (relu_and_add, h_sum, TILES), moments_of(H, D))
            invert()

            def x_plus_h(k, slot):
                return v.tensor_tensor(col(X, k, D), col(X, k, D), col(H, k, D), ALU.add)
            pipeline((times_weight(2, 2), h_scaled, TILES), (x_plus_h, x_sum, TILES), moments_of(X, D),
                     between=lambda: invert(0, FIRST_PART))
            invert(FIRST_PART, TILES)

            qe = PG[:, 0:STEPS * D_Q].rearrange("p (t w) -> p t w", w=D_Q)

            def spread(first, end):
                for c in range(D_Q):
                    v.tensor_tensor_scan(qe[:, first:end, c], keep_sum[:, first:end], qe[:, first:end, c], 0.0,
                                         ALU.mult, ALU.add).then_inc(qedge_scan, 1)

            def spread_rest():
                dve.wait_ge(qedge_in[1], 16 * 4)
                spread(Q_FIRST - 1, STEPS)
                dve.wait_ge(qedge_scan, 2 * D_Q)
            dve.wait_ge(qedge_in[0], 16)
            dve.wait_ge(qhead_in, 16)
            prep(v.tensor_copy(qe[:, 0, :], qhead[:, :]))
            spread(0, Q_FIRST)
            dve.wait_ge(qedge_scan, D_Q)
            weighted_pass(spread_rest)
            tail(3)

            w = W_STATE[3]
            inv, rr = tmp[:, 5, 0:TILES], tmp[:, 6, 0:TILES]

            def sums(g, n, at):
                return col(PG, g, 4 * w, n * w).rearrange("p (k w) -> p k w", w=w)[:, :, at:at + 1]

            def four(t, g, n):
                return col(t, g, 4, n).rearrange("p (k w) -> p k w", w=1)

            def mix(g, n, before):
                old = [(g - 1) * 4 + i for i in range(before)]
                for k in old:
                    wait(dve, mix_inv, g)
                    v.scalar_tensor_tensor(out=col(X, k, D), in0=col(PG, k, w, D), scalar=tile_of(inv, k),
                                           in1=col(X, k, D), op0=ALU.mult, op1=ALU.add).then_inc(mix_pooled, 1)
                if n:
                    for i in range(n):
                        pooled(3, g * 4 + i, i)
                    v.scalar_tensor_tensor(out=four(inv, g, n), in0=sums(g, n, D), scalar=0.01, in1=sums(g, n, D + 1),
                                           op0=ALU.add, op1=ALU.add).then_inc(mix_total, 1)
                if n:
                    wait(dve, mix_total, g + 1)
                    if not isinstance(g, int):
                        dve.sem_inc(pace)
                    v.reciprocal(four(inv, g, n), four(inv, g, n)).then_inc(mix_inv, 1)
                for k in old:
                    wait(dve, mix_pooled, k + 1)
                    wait(dve, mix_share, g)
                    v.scalar_tensor_tensor(out=col(X, k, D), in0=col(H, k, D), scalar=tile_of(rr, k),
                                           in1=col(X, k, D), op0=ALU.mult, op1=ALU.add).then_inc(x_sum, 1)
                if n:
                    wait(dve, mix_inv, g + 1)
                    v.tensor_tensor(four(rr, g, n), sums(g, n, D + 1), four(inv, g, n), ALU.mult).then_inc(mix_share, 1)
                for k in old:
                    wait(dve, x_sum, 2 * TILES + k + 1)
                    moments(X, D, k)
            mix(0, 4, 0)
            with dve.Fori(1, MEASURED // 4) as g:
                mix(g, 4, 4)
            invert(0, FIRST_PART)
            with dve.Fori(MEASURED // 4, TILES // 4) as g:
                mix(g, 4, 4)
            mix(TILES // 4, 1, 4)
            mix(TILES // 4 + 1, 0, 1)
            invert(FIRST_PART, TILES)

            def own_half(k, slot):
                product(M_S_H, k)
                wait(dve, h_norm, 4 * TILES + k + 1)
                v.tensor_tensor(col(X, k, D), mm[slot % 2][:, 0:D], col(X, k, D), ALU.add).then_inc(mm_used, 1)
            scan_pass(4, own_half)
            tail(4)

            v.tensor_copy(wedge_hi, wedge[:, :, :]).then_inc(wedge_set, 1)
            dve.wait_ge(wedge_set, 1)
            v.tensor_tensor(wedge_lo, wedge[:, :, :], wedge_hi.bitcast(f32), ALU.subtract).then_inc(wedge_set, 1)
            dve.wait_ge(w2_in, 16)
            v.tensor_copy(w2_hi, w2[:, :, :]).then_inc(wedge_set, 1)
            dve.wait_ge(wedge_set, 3)
            v.tensor_tensor(w2_lo, w2[:, :, :], w2_hi.bitcast(f32), ALU.subtract).then_inc(wedge_set, 1)

            def sage(k, slot):
                product(M_S_P, k)
                return v.scalar_tensor_tensor(out=col(X, k, D), in0=mm[slot % 2][:, 0:D], scalar=tile_of(icnt, k),
                                              in1=col(X, k, D), op0=ALU.mult, op1=ALU.add)
            pipeline((sage, mm_used, consumer(M_S_P)[1]), moments_of(X, D))
            invert()

            def low_part(k, slot):
                wait(dve, at_ready, M_EDGE * TILES + k + 1)
                wait(dve, mm_ready, M_EDGE * TILES + k - 1)
                v.tensor_tensor(hT_lo[:, slot % 2, :], tp[slot % 2][:, 0:2 * P], hT_hi[:, slot % 2, :].bitcast(f32),
                                ALU.subtract).then_inc(at_low, 1)
            tiles(dve, low_part)

            mlp_pass()
            tail(5)

            def last_sum(k, slot):
                pooled(5, k, slot)
                return v.tensor_tensor(col(H, k, D), col(PG, k, D), col(H, k, D), ALU.add)

            def summed(first, end):
                pipeline((last_sum, h_sum, 2 * TILES), moments_of(H, D), first=first, end=end)

            def finished(first, end):
                pipeline((times_weight(4, 6), h_scaled, 2 * TILES), (x_plus_h, out_dve, TILES), first=first, end=end)
            dve.wait_ge(beta_added, TILES)
            summed(0, FIRST_PART)
            invert(0, FIRST_PART)
            finished(0, FIRST_PART)
            summed(FIRST_PART, TILES)
            invert(FIRST_PART, TILES)
            finished(FIRST_PART, TILES)


def kernel(x, src, dst, edge_attr_64, **w):
    import numpy as np
    import concourse.bacc as bacc
    from concourse.bass_utils import run_bass_kernel_spmd

    def pad(a, n, value=0):
        a = np.asarray(a)
        return np.concatenate([a, np.full((n - a.shape[0],) + a.shape[1:], value, a.dtype)])

    def weights(*parts):
        a = np.concatenate([np.asarray(p) for p in parts], 0)
        return a.reshape(-1, P, a.shape[1]).transpose(1, 0, 2)

    w = {k: np.asarray(v) for k, v in w.items()}
    zero_row = np.zeros(D, np.float32)
    arrays = {
        "x": pad(x, ROWS),
        "src": pad(src, EDGES).reshape(P, GROUPS, G).transpose(1, 0, 2),
        "dst": np.lib.stride_tricks.sliding_window_view(
            pad(np.concatenate([np.full(1, -1, np.int32), np.asarray(dst)]), EDGES + 1, ROWS), STEPS + 1)[::STEPS],
        "attr": pad(pad(edge_attr_64, EDGES).reshape(P, GROUPS, G, D_EDGE).transpose(1, 3, 2, 0)
                    .reshape(GROUPS, D_EDGE, G * P), GROUPS + 1),
        "w_proj": weights(w["L0_gnn_Wp1"].T), "w_l0a": weights(w["L0_gnn_Wm1"].T),
        "w_l0b": weights(w["L0_gnn_Wm2"].T), "w_l0c": weights(w["L0_gnn_Wm3"].T),
        "w_sage": weights(w["L2_gnn_W1"].T, w["L2_gnn_W2"].T), "w_q": weights(w["L1_gnn_W_dis"].T),
        "w_edge": weights(np.concatenate([w["L3_gnn_W1"][:D], w["L3_gnn_Wg"][:D]], 1)),
        "w_attr": np.concatenate([w["L3_gnn_W1"][D:], w["L3_gnn_Wg"][D:]], 1).reshape(D_EDGE, 2, D),
        "w_2": weights(w["L3_gnn_W2"]),
        "bias": np.concatenate([w[n] for n in ("L0_gnn_bp1", "L0_gnn_bm1", "L0_gnn_bm2", "L0_gnn_bm3", "L2_gnn_b1",
                                               "L2_gnn_b2", "L3_gnn_b1", "L3_gnn_bg", "L3_gnn_b2")]).reshape(1, 9, D),
        "ln": np.stack([w[n] for n in ("L0_gnn_ln2_g", "L0_gnn_ln2_b", "L0_gnn_ln3_g", "L0_gnn_ln3_b",
                                       "L3_gnn_gamma", "L3_gnn_beta")]),
    }
    arrays = {n: np.ascontiguousarray(a) for n, a in arrays.items()}
    nc = bacc.Bacc("TRN2", target_bir_lowering=False, num_devices=1)
    dram = {n: nc.dram_tensor(f"in_{n}", a.shape, mybir.dt.from_np(a.dtype), kind="ExternalInput").ap()
            for n, a in arrays.items()}
    scratch = {"states": (EDGES + 1, D), "states_wide": (EDGES + 1, D + 2), "q_edge": (EDGES + ROWS, D_Q),
               "q_node": (ROWS, D_Q)}
    scratch.update({f"table{i}": (ROWS, W_TAB[i]) for i in range(6)})
    for n, shape in scratch.items():
        dram[n] = nc.dram_tensor(n, shape, mybir.dt.float32, kind="Internal").ap()
    out = nc.dram_tensor("out", (N_NODES, D), mybir.dt.float32, kind="ExternalOutput").ap()
    build(nc, dram, out)
    r = run_bass_kernel_spmd(nc, [{f"in_{n}": a for n, a in arrays.items()}], core_ids=[0])
    return r.results[0]["out"]
```
